# Optimizing a Trainium2 kernel written in Bass

```python
import numpy as np
import jax
import jax.numpy as jnp

def _softmax(x, axis=-1):
    return jax.nn.softmax(x, axis=axis)

def _gelu(x):
    return jax.nn.gelu(x, approximate=True)

def _silu(x):
    return jax.nn.silu(x)

def _sigmoid(x):
    return jax.nn.sigmoid(x)

def _layernorm(x, axis=-1, eps=1e-05):
    m = jnp.mean(x, axis=axis, keepdims=True)
    v = jnp.var(x, axis=axis, keepdims=True)
    return (x - m) / jnp.sqrt(v + eps)

def _scatter_add(tgt, idx, src, axis=0):
    return tgt.at[idx].add(src)

def _segment_sum(src, seg, n):
    return jax.ops.segment_sum(src, seg, n)
kernel_name = 'mk_dlrm_tower_d1_rec_r8_524a89'

def setup_inputs(seed: int=0):
    np.random.seed(seed)
    _w = jnp.asarray

    def _rec_inputs():
        import jax
        import jax.numpy as jnp
        _tk = jax.random.key(seed)
        dense_ctx = jax.random.normal(jax.random.fold_in(_tk, 190), (512, 16), jnp.float32)
        ids = jnp.stack([jax.random.randint(jax.random.fold_in(_tk, 200 + f), (512,), 0, v, jnp.int32) for f, v in enumerate([1250, 1250, 125000, 1250, 1250, 125000, 125000, 12500, 125000, 1000, 1000, 125000, 1000, 1250, 1000, 12500, 1250, 125000, 1000, 12500, 12500, 12500, 1000, 12500, 12500, 1000, 12500, 1000, 125000, 1000, 1000, 1250, 1000, 1250, 12500, 1250, 1250, 1000, 12500])], axis=1)
        tbl_0 = 0.05 * jax.random.normal(jax.random.fold_in(_tk, 500 + 0), (1250, 16), jnp.float32)
        tbl_1 = 0.05 * jax.random.normal(jax.random.fold_in(_tk, 500 + 1), (1250, 16), jnp.float32)
        tbl_2 = 0.05 * jax.random.normal(jax.random.fold_in(_tk, 500 + 2), (125000, 16), jnp.float32)
        tbl_3 = 0.05 * jax.random.normal(jax.random.fold_in(_tk, 500 + 3), (1250, 16), jnp.float32)
        tbl_4 = 0.05 * jax.random.normal(jax.random.fold_in(_tk, 500 + 4), (1250, 16), jnp.float32)
        tbl_5 = 0.05 * jax.random.normal(jax.random.fold_in(_tk, 500 + 5), (125000, 16), jnp.float32)
        tbl_6 = 0.05 * jax.random.normal(jax.random.fold_in(_tk, 500 + 6), (125000, 16), jnp.float32)
        tbl_7 = 0.05 * jax.random.normal(jax.random.fold_in(_tk, 500 + 7), (12500, 16), jnp.float32)
        tbl_8 = 0.05 * jax.random.normal(jax.random.fold_in(_tk, 500 + 8), (125000, 16), jnp.float32)
        tbl_9 = 0.05 * jax.random.normal(jax.random.fold_in(_tk, 500 + 9), (1000, 16), jnp.float32)
        tbl_10 = 0.05 * jax.random.normal(jax.random.fold_in(_tk, 500 + 10), (1000, 16), jnp.float32)
        tbl_11 = 0.05 * jax.random.normal(jax.random.fold_in(_tk, 500 + 11), (125000, 16), jnp.float32)
        tbl_12 = 0.05 * jax.random.normal(jax.random.fold_in(_tk, 500 + 12), (1000, 16), jnp.float32)
        tbl_13 = 0.05 * jax.random.normal(jax.random.fold_in(_tk, 500 + 13), (1250, 16), jnp.float32)
        tbl_14 = 0.05 * jax.random.normal(jax.random.fold_in(_tk, 500 + 14), (1000, 16), jnp.float32)
        tbl_15 = 0.05 * jax.random.normal(jax.random.fold_in(_tk, 500 + 15), (12500, 16), jnp.float32)
        tbl_16 = 0.05 * jax.random.normal(jax.random.fold_in(_tk, 500 + 16), (1250, 16), jnp.float32)
        tbl_17 = 0.05 * jax.random.normal(jax.random.fold_in(_tk, 500 + 17), (125000, 16), jnp.float32)
        tbl_18 = 0.05 * jax.random.normal(jax.random.fold_in(_tk, 500 + 18), (1000, 16), jnp.float32)
        tbl_19 = 0.05 * jax.random.normal(jax.random.fold_in(_tk, 500 + 19), (12500, 16), jnp.float32)
        tbl_20 = 0.05 * jax.random.normal(jax.random.fold_in(_tk, 500 + 20), (12500, 16), jnp.float32)
        tbl_21 = 0.05 * jax.random.normal(jax.random.fold_in(_tk, 500 + 21), (12500, 16), jnp.float32)
        tbl_22 = 0.05 * jax.random.normal(jax.random.fold_in(_tk, 500 + 22), (1000, 16), jnp.float32)
        tbl_23 = 0.05 * jax.random.normal(jax.random.fold_in(_tk, 500 + 23), (12500, 16), jnp.float32)
        tbl_24 = 0.05 * jax.random.normal(jax.random.fold_in(_tk, 500 + 24), (12500, 16), jnp.float32)
        tbl_25 = 0.05 * jax.random.normal(jax.random.fold_in(_tk, 500 + 25), (1000, 16), jnp.float32)
        tbl_26 = 0.05 * jax.random.normal(jax.random.fold_in(_tk, 500 + 26), (12500, 16), jnp.float32)
        tbl_27 = 0.05 * jax.random.normal(jax.random.fold_in(_tk, 500 + 27), (1000, 16), jnp.float32)
        tbl_28 = 0.05 * jax.random.normal(jax.random.fold_in(_tk, 500 + 28), (125000, 16), jnp.float32)
        tbl_29 = 0.05 * jax.random.normal(jax.random.fold_in(_tk, 500 + 29), (1000, 16), jnp.float32)
        tbl_30 = 0.05 * jax.random.normal(jax.random.fold_in(_tk, 500 + 30), (1000, 16), jnp.float32)
        tbl_31 = 0.05 * jax.random.normal(jax.random.fold_in(_tk, 500 + 31), (1250, 16), jnp.float32)
        tbl_32 = 0.05 * jax.random.normal(jax.random.fold_in(_tk, 500 + 32), (1000, 16), jnp.float32)
        tbl_33 = 0.05 * jax.random.normal(jax.random.fold_in(_tk, 500 + 33), (1250, 16), jnp.float32)
        tbl_34 = 0.05 * jax.random.normal(jax.random.fold_in(_tk, 500 + 34), (12500, 16), jnp.float32)
        tbl_35 = 0.05 * jax.random.normal(jax.random.fold_in(_tk, 500 + 35), (1250, 16), jnp.float32)
        tbl_36 = 0.05 * jax.random.normal(jax.random.fold_in(_tk, 500 + 36), (1250, 16), jnp.float32)
        tbl_37 = 0.05 * jax.random.normal(jax.random.fold_in(_tk, 500 + 37), (1000, 16), jnp.float32)
        tbl_38 = 0.05 * jax.random.normal(jax.random.fold_in(_tk, 500 + 38), (12500, 16), jnp.float32)
        _rk = jax.random.fold_in(_tk, 7)
        W_top1 = 0.05 * jax.random.normal(jax.random.fold_in(_tk, 801), (400, 512), jnp.float32)
        W_top2 = 0.0441942 * jax.random.normal(jax.random.fold_in(_tk, 802), (512, 256), jnp.float32)
        W_top3 = 0.0625 * jax.random.normal(jax.random.fold_in(_tk, 803), (256, 1), jnp.float32)
        b_top1 = jnp.zeros((512,), jnp.float32)
        b_top2 = jnp.zeros((256,), jnp.float32)
        return (dense_ctx, ids, tbl_0, tbl_1, tbl_2, tbl_3, tbl_4, tbl_5, tbl_6, tbl_7, tbl_8, tbl_9, tbl_10, tbl_11, tbl_12, tbl_13, tbl_14, tbl_15, tbl_16, tbl_17, tbl_18, tbl_19, tbl_20, tbl_21, tbl_22, tbl_23, tbl_24, tbl_25, tbl_26, tbl_27, tbl_28, tbl_29, tbl_30, tbl_31, tbl_32, tbl_33, tbl_34, tbl_35, tbl_36, tbl_37, tbl_38, W_top1, b_top1, W_top2, b_top2, W_top3)
    dense_ctx, ids, tbl_0, tbl_1, tbl_2, tbl_3, tbl_4, tbl_5, tbl_6, tbl_7, tbl_8, tbl_9, tbl_10, tbl_11, tbl_12, tbl_13, tbl_14, tbl_15, tbl_16, tbl_17, tbl_18, tbl_19, tbl_20, tbl_21, tbl_22, tbl_23, tbl_24, tbl_25, tbl_26, tbl_27, tbl_28, tbl_29, tbl_30, tbl_31, tbl_32, tbl_33, tbl_34, tbl_35, tbl_36, tbl_37, tbl_38, W_top1, b_top1, W_top2, b_top2, W_top3 = _rec_inputs()

    def _L0_rec_setup():
        import jax, jax.numpy as jnp
        import numpy as np
        M_FIELDS = 39
        EMB_D = 16
        UNITS = [128, 128, 128]
        BATCH = 256

        def _cin_forward(x, ws, bs):
            b, m, D = x.shape
            prev = x
            logit = []
            for k in range(len(ws)):
                h = prev.shape[1]
                z = jnp.einsum('bmd,bhd->bdmh', x, prev).reshape(b, D, m * h)
                t = jnp.einsum('bdc,co->bdo', z, ws[k]) + bs[k]
                t = jnp.transpose(t, (0, 2, 1))
                norm = jnp.sqrt(jnp.sum(t * t, axis=(-2, -1), keepdims=True))
                t = t / norm
                logit.append(t)
                prev = t
            return jnp.sum(jnp.concatenate(logit, axis=1), axis=-1)
        key = jax.random.key(seed)
        ks = jax.random.split(key, 4)
        x = jax.random.normal(ks[0], (BATCH, M_FIELDS, EMB_D), dtype=jnp.float32)
        w0 = jax.random.normal(ks[1], (M_FIELDS * M_FIELDS, UNITS[0]), dtype=jnp.float32) * 0.05
        w1 = jax.random.normal(ks[2], (UNITS[0] * M_FIELDS, UNITS[1]), dtype=jnp.float32) * 0.05
        w2 = jax.random.normal(ks[3], (UNITS[1] * M_FIELDS, UNITS[2]), dtype=jnp.float32) * 0.05
        b0 = jnp.zeros((UNITS[0],), dtype=jnp.float32)
        b1 = jnp.zeros((UNITS[1],), dtype=jnp.float32)
        b2 = jnp.zeros((UNITS[2],), dtype=jnp.float32)
        return {'x': x, 'w0': w0, 'w1': w1, 'w2': w2, 'b0': b0, 'b1': b1, 'b2': b2}
    _L0_rec_all = _L0_rec_setup()
    _L0_rec_in = {k: v for k, v in _L0_rec_all.items() if k in ('w0', 'w1', 'w2', 'b0', 'b1', 'b2')}
    del _L0_rec_all
    return {'dense_ctx': dense_ctx, 'ids': ids, 'tbl_0': tbl_0, 'tbl_1': tbl_1, 'tbl_2': tbl_2, 'tbl_3': tbl_3, 'tbl_4': tbl_4, 'tbl_5': tbl_5, 'tbl_6': tbl_6, 'tbl_7': tbl_7, 'tbl_8': tbl_8, 'tbl_9': tbl_9, 'tbl_10': tbl_10, 'tbl_11': tbl_11, 'tbl_12': tbl_12, 'tbl_13': tbl_13, 'tbl_14': tbl_14, 'tbl_15': tbl_15, 'tbl_16': tbl_16, 'tbl_17': tbl_17, 'tbl_18': tbl_18, 'tbl_19': tbl_19, 'tbl_20': tbl_20, 'tbl_21': tbl_21, 'tbl_22': tbl_22, 'tbl_23': tbl_23, 'tbl_24': tbl_24, 'tbl_25': tbl_25, 'tbl_26': tbl_26, 'tbl_27': tbl_27, 'tbl_28': tbl_28, 'tbl_29': tbl_29, 'tbl_30': tbl_30, 'tbl_31': tbl_31, 'tbl_32': tbl_32, 'tbl_33': tbl_33, 'tbl_34': tbl_34, 'tbl_35': tbl_35, 'tbl_36': tbl_36, 'tbl_37': tbl_37, 'tbl_38': tbl_38, 'W_top1': W_top1, 'b_top1': b_top1, 'W_top2': W_top2, 'b_top2': b_top2, 'W_top3': W_top3, 'L0_rec_w0': _L0_rec_in['w0'], 'L0_rec_w1': _L0_rec_in['w1'], 'L0_rec_w2': _L0_rec_in['w2'], 'L0_rec_b0': _L0_rec_in['b0'], 'L0_rec_b1': _L0_rec_in['b1'], 'L0_rec_b2': _L0_rec_in['b2']}

def reference(dense_ctx, ids, tbl_0, tbl_1, tbl_2, tbl_3, tbl_4, tbl_5, tbl_6, tbl_7, tbl_8, tbl_9, tbl_10, tbl_11, tbl_12, tbl_13, tbl_14, tbl_15, tbl_16, tbl_17, tbl_18, tbl_19, tbl_20, tbl_21, tbl_22, tbl_23, tbl_24, tbl_25, tbl_26, tbl_27, tbl_28, tbl_29, tbl_30, tbl_31, tbl_32, tbl_33, tbl_34, tbl_35, tbl_36, tbl_37, tbl_38, W_top1, b_top1, W_top2, b_top2, W_top3, L0_rec_w0, L0_rec_w1, L0_rec_w2, L0_rec_b0, L0_rec_b1, L0_rec_b2):
    import jax
    import jax.numpy as jnp

    def _L0_rec_ref(x, w0, w1, w2, b0, b1, b2):
        import jax, jax.numpy as jnp
        import numpy as np
        M_FIELDS = 39
        EMB_D = 16
        UNITS = [128, 128, 128]
        BATCH = 256

        def _cin_forward(x, ws, bs):
            b, m, D = x.shape
            prev = x
            logit = []
            for k in range(len(ws)):
                h = prev.shape[1]
                z = jnp.einsum('bmd,bhd->bdmh', x, prev).reshape(b, D, m * h)
                t = jnp.einsum('bdc,co->bdo', z, ws[k]) + bs[k]
                t = jnp.transpose(t, (0, 2, 1))
                norm = jnp.sqrt(jnp.sum(t * t, axis=(-2, -1), keepdims=True))
                t = t / norm
                logit.append(t)
                prev = t
            return jnp.sum(jnp.concatenate(logit, axis=1), axis=-1)
        return _cin_forward(x, [w0, w1, w2], [b0, b1, b2])
    e = jnp.stack([tbl_0[ids[:, 0]], tbl_1[ids[:, 1]], tbl_2[ids[:, 2]], tbl_3[ids[:, 3]], tbl_4[ids[:, 4]], tbl_5[ids[:, 5]], tbl_6[ids[:, 6]], tbl_7[ids[:, 7]], tbl_8[ids[:, 8]], tbl_9[ids[:, 9]], tbl_10[ids[:, 10]], tbl_11[ids[:, 11]], tbl_12[ids[:, 12]], tbl_13[ids[:, 13]], tbl_14[ids[:, 14]], tbl_15[ids[:, 15]], tbl_16[ids[:, 16]], tbl_17[ids[:, 17]], tbl_18[ids[:, 18]], tbl_19[ids[:, 19]], tbl_20[ids[:, 20]], tbl_21[ids[:, 21]], tbl_22[ids[:, 22]], tbl_23[ids[:, 23]], tbl_24[ids[:, 24]], tbl_25[ids[:, 25]], tbl_26[ids[:, 26]], tbl_27[ids[:, 27]], tbl_28[ids[:, 28]], tbl_29[ids[:, 29]], tbl_30[ids[:, 30]], tbl_31[ids[:, 31]], tbl_32[ids[:, 32]], tbl_33[ids[:, 33]], tbl_34[ids[:, 34]], tbl_35[ids[:, 35]], tbl_36[ids[:, 36]], tbl_37[ids[:, 37]], tbl_38[ids[:, 38]]], axis=1)
    z = _L0_rec_ref(e, L0_rec_w0, L0_rec_w1, L0_rec_w2, L0_rec_b0, L0_rec_b1, L0_rec_b2)
    z = z.reshape(z.shape[0], -1)
    h = jnp.concatenate([z, dense_ctx], axis=1)
    h = jnp.maximum(h @ W_top1 + b_top1, 0.0)
    h = jnp.maximum(h @ W_top2 + b_top2, 0.0)
    y = h @ W_top3
    return y

_drawn_inputs = setup_inputs


def setup_inputs(seed=0):
    import zlib

    import numpy as np

    out = dict(_drawn_inputs(seed))
    spreads = {'b_top1': (0.0, 0.1),
     'b_top2': (0.0, 0.1),
     'L0_rec_b0': (0.0, 0.1),
     'L0_rec_b1': (0.0, 0.1),
     'L0_rec_b2': (0.0, 0.1)}
    factors = {'tbl_0': 8.0,
     'tbl_1': 8.0,
     'tbl_2': 8.0,
     'tbl_3': 8.0,
     'tbl_4': 8.0,
     'tbl_5': 8.0,
     'tbl_6': 8.0,
     'tbl_7': 8.0,
     'tbl_8': 8.0,
     'tbl_9': 8.0,
     'tbl_10': 8.0,
     'tbl_11': 8.0,
     'tbl_12': 8.0,
     'tbl_13': 8.0,
     'tbl_14': 8.0,
     'tbl_15': 8.0,
     'tbl_16': 8.0,
     'tbl_17': 8.0,
     'tbl_18': 8.0,
     'tbl_19': 8.0,
     'tbl_20': 8.0,
     'tbl_21': 8.0,
     'tbl_22': 8.0,
     'tbl_23': 8.0,
     'tbl_24': 8.0,
     'tbl_25': 8.0,
     'tbl_26': 8.0,
     'tbl_27': 8.0,
     'tbl_28': 8.0,
     'tbl_29': 8.0,
     'tbl_30': 8.0,
     'tbl_31': 8.0,
     'tbl_32': 8.0,
     'tbl_33': 8.0,
     'tbl_34': 8.0,
     'tbl_35': 8.0,
     'tbl_36': 8.0,
     'tbl_37': 8.0,
     'tbl_38': 8.0,
     'L0_rec_w0': 5.954,
     'L0_rec_w1': 8.0,
     'L0_rec_w2': 8.0}
    for name, (base, spread) in spreads.items():
        noise = np.random.default_rng([zlib.crc32(name.encode()), seed]).standard_normal(out[name].shape)
        drawn = base * np.exp(spread * noise) if base else spread * noise
        out[name] = jnp.asarray(drawn.astype(out[name].dtype))
    for name, factor in factors.items():
        out[name] = (out[name] * factor).astype(out[name].dtype)
    return out
```

```python
import concourse.bass as bass
import numpy as np
from concourse import mybir
from contextlib import ExitStack

FIELDS = 39
EMB = 16
BATCH = 512
UNITS = 128
TOP1, TOP2 = 512, 256
CB = 32
CHUNKS = BATCH // CB
ROWS = CB * EMB
GATHERS = 10
SLOT_FIELDS = 128 // CB
LAST_SLOTS = FIELDS * CB - (GATHERS - 1) * 128

OFFSETS = (FIELDS + 1) // 2
PER_TILE = 128 // FIELDS
PAIR_TILES = -(-OFFSETS // PER_TILE)
PAIR_ROWS = PER_TILE * FIELDS
LAST_PAIR_ROWS = (OFFSETS - PER_TILE * (PAIR_TILES - 1)) * FIELDS
PAIR_OFFSETS = list(range(1, OFFSETS)) + [0]

GROUP = 3
CIN_GROUPS = [list(range(g, g + GROUP)) for g in range(0, FIELDS, GROUP)]
PAIR_GROUPS = [[0, 1], [2, 3], [4, 5], [6]]
NG, NP = len(CIN_GROUPS), len(PAIR_GROUPS)
PER_BODY = NG + NP + NG
RING = 5
assert PER_BODY % RING == 0 and FIELDS % GROUP == 0
SCRATCH_FIELDS = FIELDS + 5 * SLOT_FIELDS


def cin_kernel(nc, idx_in, base_in, table, ctx_t, w0a, w0b, w1, w2, b0, b1, b2,
               w_top1, b_top1, w_top2, b_top2, w_top3, out):
    f32, i32 = mybir.dt.float32, mybir.dt.int32
    ALU, ACT, AX = mybir.AluOpType, mybir.ActivationFunctionType, mybir.AxisListType
    F32_MAX = float(np.finfo(np.float32).max)

    scratch = nc.dram_tensor("x_scratch", [CHUNKS, SCRATCH_FIELDS * CB, EMB], f32, kind="Internal").ap()

    with ExitStack() as ctx:
        def sb(name, shape, dt=f32):
            return ctx.enter_context(nc.sbuf_tensor(name, shape, dt))

        def pb(name):
            return ctx.enter_context(nc.psum_tensor(name, [128, 512], f32))

        def sem(name):
            return ctx.enter_context(nc.semaphore(name))

        ids_sb = sb("ids_sb", [128, CHUNKS * GATHERS], i32)
        base_sb = sb("base_sb", [128, GATHERS], i32)
        idx = sb("idx", [128, 2, GATHERS], i32)
        gathered = sb("gathered", [128, 2, GATHERS, EMB])
        x_rep = sb("x_rep", [128, ROWS])
        x_rot = sb("x_rot", [128, PAIR_TILES, ROWS])
        x_all = sb("x_all", [128, FIELDS, ROWS])
        z = sb("z", [128, RING, GROUP, ROWS])
        t = sb("t", [128, 3, ROWS])
        u = sb("u", [128, 3, ROWS])
        ssq = sb("ssq", [128, 3, CB])
        dsum = sb("dsum", [128, 3, CB])
        root = sb("root", [128, 3, CB])
        r = sb("r", [128, 3, CB])
        ra = sb("ra", [128, 3, CB])
        rb = sb("rb", [128, 3, CB])
        rc = sb("rc", [128, 3, CB])
        h0 = sb("h0", [128, 3 * BATCH])
        ones = sb("ones", [128, 128])
        w0_sb = sb("w0_sb", [128, PAIR_TILES, UNITS])
        w_sb = {1: sb("w1_sb", [128, FIELDS, UNITS]), 2: sb("w2_sb", [128, FIELDS, UNITS])}
        bias = sb("bias", [128, 3])
        top1_sb = sb("top1_sb", [128, 3, TOP1])
        top1c_sb = sb("top1c_sb", [EMB, TOP1])
        ctx_sb = sb("ctx_sb", [EMB, BATCH])
        top2_sb = sb("top2_sb", [128, TOP1 // 128, TOP2])
        top3_sb = sb("top3_sb", [128, TOP2 // 128])
        btop1_sb = sb("btop1_sb", [128, TOP1 // 128])
        btop2_sb = sb("btop2_sb", [128, TOP2 // 128])
        w0b_sb = z[:, RING - 1, 0:2, :].rearrange("p a (b o) -> p (a b) o", o=UNITS)
        h1 = x_all[:, 0:TOP1 // 128, :]
        h2 = x_all[:, TOP1 // 128:TOP1 // 128 + TOP2 // 128, :]
        y_sb = x_all[0:1, TOP1 // 128 + TOP2 // 128, :]

        acc = [pb("acc0"), pb("acc1"), pb("acc2")]
        norm2 = pb("norm2")
        top_ps = [pb(f"top{n}") for n in range(TOP1 // 128)]

        ids_loaded = sem("ids_loaded")
        idx_made = sem("idx_made")
        gather_done = sem("gather_done")
        scratch_written = sem("scratch_written")
        pairs_loaded = sem("pairs_loaded")
        fields_loaded = [sem(f"fields_loaded{g}") for g in range(NG)]
        w0_loaded = sem("w0_loaded")
        w0_folded = sem("w0_folded")
        bias_loaded = sem("bias_loaded")
        w_loaded = {1: sem("w1_loaded"), 2: sem("w2_loaded")}
        top_loaded = sem("top_loaded")
        ones_made = sem("ones_made")
        z_ready = sem("z_ready")
        z_used = sem("z_used")
        scaled = [None, sem("scaled1"), sem("scaled2")]
        biased = [sem(f"biased{k}") for k in range(3)]
        squared = [sem(f"squared{k}") for k in range(3)]
        summed = [sem(f"summed{k}") for k in range(3)]
        norm_done = sem("norm_done")
        root_done = sem("root_done")
        r_step = sem("r_step")
        h_ready = sem("h_ready")
        h1_ps = sem("h1_ps")
        h1_done = sem("h1_done")
        h2_ps = sem("h2_ps")
        h2_done = sem("h2_done")
        y_ps = sem("y_ps")
        y_done = sem("y_done")
        y_stored = sem("y_stored")

        R_STEPS = 4

        def group_no(body, i):
            return body * PER_BODY + (NP + i)

        def groups_through(k, chunk):
            if k == 1:
                return group_no(chunk, NG)
            if k == 0:
                return NP if isinstance(chunk, int) and chunk == 0 else group_no(chunk - 1, NG + NP)
            return group_no(chunk, PER_BODY) - (NP if isinstance(chunk, int) and chunk == CHUNKS - 1 else 0)

        def over_bodies(eng, body):
            body(0, True, False)
            with eng.Fori(1, CHUNKS - 1) as c:
                body(c, False, False)
            body(CHUNKS - 1, False, True)

        block = ctx.enter_context(nc.Block())

        @block.gpsimd
        def _(pool):
            nc.gpsimd.memset(ones[:, :], 1.0).then_inc(ones_made, 1)

            def make_rows(c, parity):
                nc.gpsimd.tensor_tensor(out=idx[:, parity, :], in0=ids_sb[:, bass.ds(c * GATHERS, GATHERS)],
                                        in1=base_sb[:, :], op=ALU.add).then_inc(idx_made, 1)

            def gather_chunk(c, parity, last=False):
                if not (isinstance(c, int) and c < 1):
                    pool.wait_ge(gather_done, c * (16 * GATHERS))
                if not (isinstance(c, int) and c < 2):
                    pool.wait_ge(scratch_written, (c - 1) * 48)
                pool.wait_ge(idx_made, c + 1)
                if not last:
                    make_rows(c + 1, 1 - parity)
                for j in range(GATHERS):
                    n = 128 if j < GATHERS - 1 else LAST_SLOTS
                    nc.gpsimd.indirect_dma_start(
                        out=gathered[0:n, parity, j, :], out_offset=None, in_=table[:, :],
                        in_offset=bass.IndirectOffsetOnAxis(ap=idx[0:n, parity, j:j + 1], axis=0)
                    ).then_inc(gather_done, 16)

            pool.wait_ge(ids_loaded, 32)
            make_rows(0, 0)
            gather_chunk(0, 0)
            gather_chunk(1, 1)
            with pool.Fori(2, CHUNKS - 3, 2) as c:
                gather_chunk(c, 0)
                gather_chunk(c + 1, 1)
            gather_chunk(CHUNKS - 2, 0)
            gather_chunk(CHUNKS - 1, 1, last=True)

        @block.sync
        def _(sp):
            def store_chunk(c, parity):
                g = gathered[:, parity, :, :]
                dst = scratch[bass.ds(c, 1), :, :].rearrange("c n e -> (c n) e")
                full = (GATHERS - 1) * 128
                sp.dma_start(dst[0:full, :].rearrange("(j p) e -> p j e", p=128),
                             g[:, 0:GATHERS - 1, :]).then_inc(scratch_written, 16)
                sp.dma_start(dst[full:full + LAST_SLOTS, :].rearrange("(j p) e -> p j e", p=LAST_SLOTS),
                             g[0:LAST_SLOTS, GATHERS - 1:GATHERS, :]).then_inc(scratch_written, 16)
                sp.dma_start(dst[FIELDS * CB:SCRATCH_FIELDS * CB, :].rearrange("(j p) e -> p j e", p=128),
                             g[:, 0:5, :]).then_inc(scratch_written, 16)

            def chunk_rows(c):
                return scratch[bass.ds(c, 1), :, :].rearrange("c (m b) e -> (c m) (b e)", b=CB)

            def load_pairs(c):
                rows = chunk_rows(c)
                for kk in range(PER_TILE):
                    at = slice(kk * FIELDS, (kk + 1) * FIELDS)
                    sp.dma_start(x_rep[at, :], rows[0:FIELDS, :]).then_inc(pairs_loaded, 16)
                    tiles = [PAIR_TILES, PAIR_TILES - 1, PAIR_TILES - 1][kk]
                    first = rows[1 + kk:1 + kk + FIELDS, :]
                    window = bass.AP(first.tensor, first.offset,
                                     [[ROWS, FIELDS], [PER_TILE * ROWS, tiles], [1, ROWS]])
                    sp.dma_start(x_rot[at, 0:tiles, :], window).then_inc(pairs_loaded, 16)
                sp.dma_start(x_rot[FIELDS:2 * FIELDS, PAIR_TILES - 1, :],
                             rows[0:FIELDS, :]).then_inc(pairs_loaded, 16)

            def load_fields(c, g):
                rows = chunk_rows(c)[g * GROUP:(g + 1) * GROUP, :].rearrange("m n -> (m n)")
                sp.dma_start(x_all[:, g * GROUP:(g + 1) * GROUP, :].rearrange("p m n -> p (m n)"),
                             rows.partition_broadcast(128)).then_inc(fields_loaded[g], 16)

            sp.dma_start(ids_sb[:, :], idx_in).then_inc(ids_loaded, 16)
            sp.dma_start(base_sb[:, :], base_in).then_inc(ids_loaded, 16)
            sp.wait_ge(gather_done, 16 * GATHERS)
            store_chunk(0, 0)
            sp.wait_ge(scratch_written, 48)
            load_pairs(0)
            for g in range(NG):
                load_fields(0, g)
            sp.wait_ge(gather_done, 2 * 16 * GATHERS)
            store_chunk(1, 1)

            def next_chunk(c, more, parity=0):
                sp.wait_ge(scratch_written, (c + 2) * 48)
                sp.wait_ge(z_ready, c * PER_BODY + (NP if isinstance(c, int) and c == 0 else NP - NG))
                load_pairs(c + 1)
                for g in range(NG):
                    sp.wait_ge(z_ready, group_no(c, NG + NP + g + 1))
                    load_fields(c + 1, g)
                if more:
                    sp.wait_ge(gather_done, (c + 3) * (16 * GATHERS))
                    store_chunk(c + 2, parity)

            next_chunk(0, True)
            with sp.Fori(1, CHUNKS - 3, 2) as c:
                next_chunk(c, True, 1)
                next_chunk(c + 1, True, 0)
            next_chunk(CHUNKS - 3, True, 1)
            next_chunk(CHUNKS - 2, False)
            sp.wait_ge(y_done, 1)
            sp.dma_start(out, y_sb[:, :]).then_inc(y_stored, 16)
            sp.wait_ge(y_stored, 16)

        @block.scalar
        def _(act):
            act.dma_start(w0_sb[0:PAIR_ROWS, :, :], w0a).then_inc(w0_loaded, 16)
            act.dma_start(w0b_sb[0:PAIR_ROWS, 0:PAIR_TILES, :], w0b).then_inc(w0_loaded, 16)
            for k, b in enumerate((b0, b1, b2)):
                act.dma_start(bias[:, k:k + 1], b).then_inc(bias_loaded, 16)
            for k, w in ((1, w1), (2, w2)):
                act.dma_start(w_sb[k][:, :, :], w.rearrange("(m h) o -> h m o", h=UNITS)).then_inc(w_loaded[k], 16)
            act.dma_start(top1_sb[:, :, :], w_top1[0:3 * 128, :].rearrange("(k p) n -> p k n", p=128)).then_inc(top_loaded, 16)
            act.dma_start(top1c_sb[:, :], w_top1[3 * 128:3 * 128 + EMB, :]).then_inc(top_loaded, 16)
            act.dma_start(ctx_sb[:, :], ctx_t).then_inc(top_loaded, 16)
            act.dma_start(top2_sb[:, :, :], w_top2.rearrange("(k p) n -> p k n", p=128)).then_inc(top_loaded, 16)
            act.dma_start(top3_sb[:, :], w_top3).then_inc(top_loaded, 16)
            act.dma_start(btop1_sb[:, :], b_top1).then_inc(top_loaded, 16)
            act.dma_start(btop2_sb[:, :], b_top2).then_inc(top_loaded, 16)
            act.wait_ge(bias_loaded, 48)

            def finish(k, c):
                if k == 0:
                    act.wait_ge(z_used, groups_through(0, c))
                    src = acc[0][:, :]
                else:
                    act.wait_ge(scaled[k], c + 1)
                    src = u[:, k, :]
                nc.scalar.activation(t[:, k, :], src, ACT.Identity, bias=bias[:, k:k + 1]).then_inc(biased[k], 1)
                act.wait_ge(biased[k], c + 1)
                if k == 0 and not (isinstance(c, int) and c == 0):
                    act.wait_ge(summed[0], c)
                nc.scalar.activation(u[:, k, :], t[:, k, :], ACT.Square).then_inc(squared[k], 1)

            def roots(n, ks):
                act.wait_ge(norm_done, n + 1)
                if not (isinstance(n, int) and n == 0):
                    act.wait_ge(r_step, n * R_STEPS)
                nc.scalar.activation(root[:, ks[0]:ks[-1] + 1, :],
                                     norm2[:, ks[0] * CB:(ks[-1] + 1) * CB].rearrange("p (k b) -> p k b", b=CB),
                                     ACT.Sqrt).then_inc(root_done, 1)

            def body(c, first, last):
                if not first:
                    finish(2, c - 1)
                finish(1, c)
                if not last:
                    finish(0, c + 1)
                roots(c + 1, [k for k in range(3) if not (k == 0 and last) and not (k == 2 and first)])

            finish(0, 0)
            roots(0, [0])
            over_bodies(act, body)
            finish(2, CHUNKS - 1)
            roots(CHUNKS + 1, [2])

            act.wait_ge(top_loaded, 7 * 16)
            for n in range(TOP1 // 128):
                act.wait_ge(h1_ps, n + 1)
                nc.scalar.activation(h1[:, n, :], top_ps[n][:, :], ACT.Relu, bias=btop1_sb[:, n:n + 1]).then_inc(h1_done, 1)
            for n in range(TOP2 // 128):
                act.wait_ge(h2_ps, n + 1)
                nc.scalar.activation(h2[:, n, :], acc[n][:, :], ACT.Relu, bias=btop2_sb[:, n:n + 1]).then_inc(h2_done, 1)
            act.wait_ge(y_ps, 1)
            nc.scalar.copy(y_sb[:, :], acc[2][0:1, :]).then_inc(y_done, 1)

        @block.tensor
        def _(pe):
            def use_group(c, i, k, tiles, chunk):
                g = group_no(c, i)
                slot = (NP + i) % RING
                total = PAIR_TILES if k == 0 else FIELDS
                if tiles[0] == 0 and not (isinstance(chunk, int) and chunk == 0):
                    pe.wait_ge(biased[0] if k == 0 else scaled[k], chunk)
                pe.wait_ge(z_ready, g + 1)
                for j, tile in enumerate(tiles):
                    rows = 128 if k else (LAST_PAIR_ROWS if tile == PAIR_TILES - 1 else PAIR_ROWS)
                    w = w_sb[k] if k else w0_sb
                    mm = nc.tensor.matmul(acc[k][:, :], w[0:rows, tile, :], z[0:rows, slot, j, :],
                                          start=(tile == 0), stop=(tile == total - 1))
                    if j == len(tiles) - 1:
                        mm.then_inc(z_used, 1)

            def norms(n, ks, chunks):
                for k, ch in zip(ks, chunks):
                    pe.wait_ge(summed[k], ch + 1)
                if not (isinstance(n, int) and n == 0):
                    pe.wait_ge(r_step, n * R_STEPS)
                nc.tensor.matmul(norm2[:, ks[0] * CB:(ks[-1] + 1) * CB], ones[:, :],
                                 ssq[:, ks[0]:ks[-1] + 1, :].rearrange("p k b -> p (k b)"),
                                 start=True, stop=True).then_inc(norm_done, 1)

            def body(c, first, last):
                if first:
                    pe.wait_ge(w_loaded[1], 16)
                for i, tiles in enumerate(CIN_GROUPS):
                    use_group(c, i, 1, tiles, c)
                if not last:
                    for i, tiles in enumerate(PAIR_GROUPS):
                        use_group(c, NG + i, 0, tiles, c + 1)
                skip = NP if last else 0
                if first:
                    pe.wait_ge(w_loaded[2], 16)
                for i, tiles in enumerate(CIN_GROUPS):
                    use_group(c, NG + NP - skip + i, 2, tiles, c)
                    if i == 5:
                        ks = [k for k in range(3) if not (k == 0 and last) and not (k == 2 and first)]
                        norms(c + 1, ks, [c + 1 - k for k in ks])

            pe.wait_ge(w0_folded, 2)
            pe.wait_ge(ones_made, 1)
            for i, tiles in enumerate(PAIR_GROUPS):
                use_group(0, i - NP, 0, tiles, 0)
            norms(0, [0], [0])
            over_bodies(pe, body)
            norms(CHUNKS + 1, [2], [CHUNKS - 1])

            pe.wait_ge(top_loaded, 7 * 16)
            parts = [(top1c_sb[:, :], ctx_sb[:, :])] + \
                    [(top1_sb[:, k, :], h0[:, k * BATCH:(k + 1) * BATCH]) for k in range(3)]
            for k, (w, x) in enumerate(parts):
                if k == 1:
                    pe.wait_ge(h_ready, CHUNKS + 1)
                if k == 3:
                    pe.wait_ge(h_ready, CHUNKS + 2)
                for n in range(TOP1 // 128):
                    mm = nc.tensor.matmul(top_ps[n][:, :], w[:, n * 128:(n + 1) * 128], x,
                                          start=(k == 0), stop=(k == 3))
                    if k == 3:
                        mm.then_inc(h1_ps, 1)
            for k in range(TOP1 // 128):
                pe.wait_ge(h1_done, k + 1)
                for n in range(TOP2 // 128):
                    mm = nc.tensor.matmul(acc[n][:, :], top2_sb[:, k, n * 128:(n + 1) * 128], h1[:, k, :],
                                          start=(k == 0), stop=(k == TOP1 // 128 - 1))
                    if k == TOP1 // 128 - 1:
                        mm.then_inc(h2_ps, 1)
            for k in range(TOP2 // 128):
                pe.wait_ge(h2_done, k + 1)
                mm = nc.tensor.matmul(acc[2][0:1, :], top3_sb[:, k:k + 1], h2[:, k, :],
                                      start=(k == 0), stop=(k == TOP2 // 128 - 1))
            mm.then_inc(y_ps, 1)

        @block.vector
        def _(dve):
            def make_group(c, i, k, tiles, chunk):
                g = group_no(c, i)
                slot = (NP + i) % RING
                n = len(tiles)
                if not (isinstance(g, int) and g < RING):
                    dve.wait_ge(z_used, g + 1 - RING)
                if k == 0:
                    if tiles[0] == 0:
                        dve.wait_ge(pairs_loaded, (chunk + 1) * (7 * 16))
                    rows = LAST_PAIR_ROWS if tiles[-1] == PAIR_TILES - 1 else PAIR_ROWS
                    a = x_rep[0:rows, :]
                    b = x_rot[0:rows, tiles[0]:tiles[0] + n, :]
                else:
                    if k == 1:
                        dve.wait_ge(fields_loaded[i], (chunk + 1) * 16)
                    if tiles[0] == 0:
                        dve.wait_ge(biased[k - 1], chunk + 1)
                    rows = 128
                    a = t[:, k - 1, :]
                    b = x_all[:, tiles[0]:tiles[0] + n, :]
                nc.vector.tensor_tensor(out=z[0:rows, slot, 0:n, :], in0=a.unsqueeze(1).to_broadcast([rows, n, ROWS]),
                                        in1=b, op=ALU.mult).then_inc(z_ready, 1)

            def scale(k, c, n):
                dve.wait_ge(z_used, groups_through(k, c))
                dve.wait_ge(r_step, n * R_STEPS)
                nc.vector.tensor_tensor(
                    out=u[:, k, :].rearrange("p (b e) -> p b e", e=EMB),
                    in0=acc[k][:, :].rearrange("p (b e) -> p b e", e=EMB),
                    in1=r[:, k - 1, :].unsqueeze(2).to_broadcast([128, CB, EMB]), op=ALU.mult).then_inc(scaled[k], 1)

            def sums(k, c):
                dve.wait_ge(biased[k], c + 1)
                nc.vector.tensor_reduce(dsum[:, k, :], t[:, k, :].rearrange("p (b e) -> p b e", e=EMB), AX.X, ALU.add)
                dve.wait_ge(squared[k], c + 1)
                nc.vector.tensor_reduce(ssq[:, k, :], u[:, k, :].rearrange("p (b e) -> p b e", e=EMB),
                                        AX.X, ALU.add).then_inc(summed[k], 1)

            def reciprocals(n, ks):
                s = slice(ks[0], ks[-1] + 1)
                sq = norm2[:, ks[0] * CB:(ks[-1] + 1) * CB].rearrange("p (k b) -> p k b", b=CB)
                dve.wait_ge(root_done, n + 1)
                nc.vector.reciprocal(ra[:, s, :], root[:, s, :]).then_inc(r_step, 1)
                dve.wait_ge(r_step, n * R_STEPS + 1)
                nc.vector.scalar_tensor_tensor(out=rb[:, s, :], in0=sq, scalar=F32_MAX, in1=ra[:, s, :],
                                               op0=ALU.min, op1=ALU.mult).then_inc(r_step, 1)
                dve.wait_ge(r_step, n * R_STEPS + 2)
                nc.vector.scalar_tensor_tensor(out=rc[:, s, :], in0=rb[:, s, :], scalar=-0.5, in1=ra[:, s, :],
                                               op0=ALU.mult, op1=ALU.mult).then_inc(r_step, 1)
                dve.wait_ge(r_step, n * R_STEPS + 3)
                nc.vector.scalar_tensor_tensor(out=r[:, s, :], in0=rc[:, s, :], scalar=1.5, in1=ra[:, s, :],
                                               op0=ALU.add, op1=ALU.mult).then_inc(r_step, 1)
                dve.wait_ge(r_step, n * R_STEPS + 4)
                k0 = ks[0]
                feats = h0[:, bass.ds(n * CB + k0 * (BATCH - CB), (len(ks) - 1) * (BATCH - CB) + CB)]
                feats = bass.AP(feats.tensor, feats.offset, [feats.ap[0], [BATCH - CB, len(ks)], [1, CB]])
                nc.vector.tensor_tensor(out=feats, in0=r[:, s, :], in1=dsum[:, s, :], op=ALU.mult).then_inc(h_ready, 1)

            def body(c, first, last):
                for i, tiles in enumerate(CIN_GROUPS):
                    make_group(c, i, 1, tiles, c)
                    if i == 3 and not first:
                        scale(2, c - 1, c + 1)
                    if i == 5 and not first:
                        sums(2, c - 1)
                if not last:
                    for i, tiles in enumerate(PAIR_GROUPS):
                        make_group(c, NG + i, 0, tiles, c + 1)
                skip = NP if last else 0
                scale(1, c, c + 1)
                ks = [k for k in range(3) if not (k == 0 and last) and not (k == 2 and first)]
                for i, tiles in enumerate(CIN_GROUPS):
                    make_group(c, NG + NP - skip + i, 2, tiles, c)
                    if i == 1:
                        sums(1, c)
                    if i == 3 and not last:
                        sums(0, c + 1)
                    if i == 10:
                        reciprocals(c + 1, ks)

            dve.wait_ge(w0_loaded, 32)
            full = slice(0, PAIR_TILES - 1)
            nc.vector.tensor_tensor(out=w0_sb[0:PAIR_ROWS, full, :], in0=w0_sb[0:PAIR_ROWS, full, :],
                                    in1=w0b_sb[0:PAIR_ROWS, full, :], op=ALU.add).then_inc(w0_folded, 1)
            nc.vector.tensor_tensor(out=w0_sb[0:FIELDS, PAIR_TILES - 1, :], in0=w0_sb[0:FIELDS, PAIR_TILES - 1, :],
                                    in1=w0b_sb[0:FIELDS, PAIR_TILES - 1, :], op=ALU.add).then_inc(w0_folded, 1)
            dve.wait_ge(w0_folded, 2)
            for i, tiles in enumerate(PAIR_GROUPS):
                make_group(0, i - NP, 0, tiles, 0)
            sums(0, 0)
            reciprocals(0, [0])
            over_bodies(dve, body)
            scale(2, CHUNKS - 1, CHUNKS + 1)
            sums(2, CHUNKS - 1)
            reciprocals(CHUNKS + 1, [2])


def kernel(**inputs):
    import concourse.bacc as bacc
    from concourse.bass_utils import run_bass_kernel_spmd

    def lay(a):
        return np.ascontiguousarray(a)

    tables = [np.asarray(inputs[f"tbl_{f}"]) for f in range(FIELDS)]
    starts = np.concatenate([[0], np.cumsum([a.shape[0] for a in tables])])[:FIELDS].astype(np.int32)
    slot_fields = GATHERS * SLOT_FIELDS

    def slots(a):
        a = a.reshape(CHUNKS, CB, FIELDS).transpose(0, 2, 1)
        a = np.concatenate([a, np.zeros((CHUNKS, slot_fields - FIELDS, CB), a.dtype)], axis=1)
        a = a.reshape(CHUNKS, GATHERS, SLOT_FIELDS * CB)
        return lay(a.transpose(2, 0, 1).reshape(128, CHUNKS * GATHERS))

    order_a = np.zeros((PAIR_ROWS, PAIR_TILES), np.int64)
    order_b = np.zeros((PAIR_ROWS, PAIR_TILES), np.int64)
    for n, k in enumerate(PAIR_OFFSETS):
        for i in range(FIELDS):
            j = (i + k) % FIELDS
            at = (n % PER_TILE * FIELDS + i, n // PER_TILE)
            order_a[at], order_b[at] = i * FIELDS + j, j * FIELDS + i
    w0 = np.asarray(inputs["L0_rec_w0"])

    arrays = {
        "ids": slots(np.asarray(inputs["ids"])),
        "bases": lay(slots(np.broadcast_to(starts, (BATCH, FIELDS)))[:, 0:GATHERS]),
        "table": lay(np.concatenate(tables, axis=0)),
        "ctx_t": lay(np.asarray(inputs["dense_ctx"]).T),
        "w0a": lay(w0[order_a]),
        "w0b": lay(w0[order_b]),
        "w1": lay(inputs["L0_rec_w1"]),
        "w2": lay(inputs["L0_rec_w2"]),
        "b0": lay(np.asarray(inputs["L0_rec_b0"]).reshape(UNITS, 1)),
        "b1": lay(np.asarray(inputs["L0_rec_b1"]).reshape(UNITS, 1)),
        "b2": lay(np.asarray(inputs["L0_rec_b2"]).reshape(UNITS, 1)),
        "w_top1": lay(inputs["W_top1"]),
        "b_top1": lay(np.asarray(inputs["b_top1"]).reshape(TOP1 // 128, 128).T),
        "w_top2": lay(inputs["W_top2"]),
        "b_top2": lay(np.asarray(inputs["b_top2"]).reshape(TOP2 // 128, 128).T),
        "w_top3": lay(np.asarray(inputs["W_top3"]).reshape(TOP2 // 128, 128).T),
    }
    nc = bacc.Bacc("TRN2", target_bir_lowering=False, num_devices=1)
    args = [nc.dram_tensor(f"in_{name}", a.shape, mybir.dt.from_np(a.dtype), kind="ExternalInput").ap()
            for name, a in arrays.items()]
    args.append(nc.dram_tensor("scores", (1, BATCH), mybir.dt.float32, kind="ExternalOutput").ap())
    cin_kernel(nc, *args)
    got = run_bass_kernel_spmd(nc, [{f"in_{name}": a for name, a in arrays.items()}], core_ids=[0])
    return got.results[0]["scores"].reshape(BATCH, 1)
```

```python
import concourse.bass as bass
import numpy as np
from concourse import mybir
from contextlib import ExitStack

FIELDS = 39
EMB = 16
BATCH = 512
UNITS = 128
TOP1, TOP2 = 512, 256
CB = 32
CHUNKS = BATCH // CB
ROWS = CB * EMB
GATHERS = 10
SLOT_FIELDS = 128 // CB
LAST_SLOTS = FIELDS * CB - (GATHERS - 1) * 128

OFFSETS = (FIELDS + 1) // 2
PER_TILE = 128 // FIELDS
PAIR_TILES = -(-OFFSETS // PER_TILE)
PAIR_ROWS = PER_TILE * FIELDS
LAST_PAIR_ROWS = (OFFSETS - PER_TILE * (PAIR_TILES - 1)) * FIELDS
PAIR_OFFSETS = list(range(1, OFFSETS)) + [0]

GROUP = 3
CIN_GROUPS = [list(range(g, g + GROUP)) for g in range(0, FIELDS, GROUP)]
PAIR_GROUPS = [[0, 1], [2, 3], [4, 5], [6]]
NG, NP = len(CIN_GROUPS), len(PAIR_GROUPS)
PER_BODY = NG + NP + NG
RING = 5

SPLITS_IN_GROUP = [2, 1, 2, 2, 1, 2, 2, 1, 2, 2, 1, 2, 0]
SPLIT_FIELDS = [GROUP * (g + 1) - 1 - n for g in range(NG) for n in reversed(range(SPLITS_IN_GROUP[g]))]
WHOLE_FIELDS = [m for m in range(FIELDS) if m not in SPLIT_FIELDS]
WEIGHT_ORDER = SPLIT_FIELDS + WHOLE_FIELDS
SPLIT = len(SPLIT_FIELDS)
SPLIT_SLOTS = 4
DMA_SCRATCH = 8192
SPLIT_SEQ = [(k, n) for k in (1, 2) for n in range(SPLIT)]
LOW_ON_VECTOR = [n % 5 == 4 for n in range(SPLIT)]
STAGE_TILES = -(-SPLIT * UNITS // ROWS)
assert len(SPLIT_SEQ) % SPLIT_SLOTS == 0
assert PER_BODY % RING == 0 and FIELDS % GROUP == 0
SCRATCH_FIELDS = FIELDS + 5 * SLOT_FIELDS


def cin_kernel(nc, idx_in, base_in, table, ctx_t, w0a, w0b, w1, w2, b0, b1, b2,
               w_top1, b_top1, w_top2, b_top2, w_top3, out):
    f32, f32r, i32 = mybir.dt.float32, mybir.dt.float32r, mybir.dt.int32
    ALU, ACT, AX = mybir.AluOpType, mybir.ActivationFunctionType, mybir.AxisListType
    F32_MAX = float(np.finfo(np.float32).max)

    scratch = nc.dram_tensor("x_scratch", [CHUNKS, SCRATCH_FIELDS * CB, EMB], f32, kind="Internal").ap()

    with ExitStack() as ctx:
        def sb(name, shape, dt=f32):
            return ctx.enter_context(nc.sbuf_tensor(name, shape, dt))

        def pb(name):
            return ctx.enter_context(nc.psum_tensor(name, [128, 512], f32))

        def sem(name):
            return ctx.enter_context(nc.semaphore(name))

        ids_sb = sb("ids_sb", [128, CHUNKS * GATHERS], i32)
        base_sb = sb("base_sb", [128, GATHERS], i32)
        idx = sb("idx", [128, 2, GATHERS], i32)
        gathered = sb("gathered", [128, 2, GATHERS, EMB])
        x_rep = sb("x_rep", [128, ROWS])
        x_rot = sb("x_rot", [128, PAIR_TILES, ROWS])
        x_all = sb("x_all", [128, FIELDS, ROWS])
        z = sb("z", [128, RING, GROUP, ROWS])
        ht = sb("ht", [128, 4, ROWS])
        h0 = ht[:, 0:3, :].rearrange("p k n -> p (k n)")
        ssq = sb("ssq", [128, 3, CB])
        dsum = sb("dsum", [128, 3, CB])
        root = sb("root", [128, 3, CB])
        r = sb("r", [128, 3, CB])
        ra = sb("ra", [128, 3, CB])
        rb = sb("rb", [128, 3, CB])
        rc = sb("rc", [128, 3, CB])
        ones = sb("ones", [128, 128])
        w0_sb = sb("w0_sb", [128, PAIR_TILES, UNITS])
        w_sb = {k: sb(f"w{k}_sb", [128, len(WHOLE_FIELDS), UNITS]) for k in (1, 2)}
        w_hi = {k: sb(f"w{k}_hi", [128, SPLIT, UNITS], f32r) for k in (1, 2)}
        w_lo = {k: sb(f"w{k}_lo", [128, SPLIT, UNITS], f32r) for k in (1, 2)}
        z_hi = sb("z_hi", [128, SPLIT_SLOTS, ROWS], f32r)
        z_lo = sb("z_lo", [128, SPLIT_SLOTS, ROWS], f32r)
        bias = sb("bias", [128, 3])
        top3_sb = sb("top3_sb", [128, TOP2 // 128])
        btop1_sb = sb("btop1_sb", [128, TOP1 // 128])
        btop2_sb = sb("btop2_sb", [128, TOP2 // 128])
        z_tiles = z[:, :, :, :].rearrange("p s j n -> p (s j) n")
        w0b_sb = z_tiles[:, RING * GROUP - 2:RING * GROUP, :].rearrange("p a (b o) -> p (a b) o", o=UNITS)
        w_raw = {k: x_all[:, FIELDS - k * STAGE_TILES:FIELDS - (k - 1) * STAGE_TILES, :]
                 .rearrange("p a (b o) -> p (a b) o", o=UNITS)[:, 0:SPLIT, :] for k in (1, 2)}
        h1 = x_all[:, 0:TOP1 // 128, :]
        h2 = x_all[:, TOP1 // 128:TOP1 // 128 + TOP2 // 128, :]
        y_sb = x_all[0:1, 6, :]
        top1_sb = x_all[:, 7:10, :]
        top1c_sb = x_all[0:EMB, 10, :]
        ctx_sb = x_all[0:EMB, 11, :]
        top2_sb = x_all[:, 12:14, :].rearrange("p a (b n) -> p (a b) n", n=TOP2)

        acc = [pb("acc0"), pb("acc1"), pb("acc2")]
        norm2 = pb("norm2")
        top_ps = [pb(f"top{n}") for n in range(TOP1 // 128)]
        u = [top_ps[0], top_ps[1], norm2]
        t = [top_ps[2][:, :], top_ps[3][:, :], ht[:, 3, :]]

        ids_loaded = sem("ids_loaded")
        idx_made = sem("idx_made")
        gather_done = sem("gather_done")
        scratch_written = sem("scratch_written")
        pairs_loaded = sem("pairs_loaded")
        fields_loaded = [sem(f"fields_loaded{g}") for g in range(NG)]
        w0_loaded = sem("w0_loaded")
        w0_folded = sem("w0_folded")
        bias_loaded = sem("bias_loaded")
        w_loaded = {1: sem("w1_loaded"), 2: sem("w2_loaded")}
        top_loaded = sem("top_loaded")
        top_bias_loaded = sem("top_bias_loaded")
        w_split_loaded = {k: sem(f"w{k}_split_loaded") for k in (1, 2)}
        w_hi_made = sem("w_hi_made")
        w_lo_made = sem("w_lo_made")
        hi_ready = sem("hi_ready")
        lo_ready_pool = sem("lo_ready_pool")
        lo_ready_vector = sem("lo_ready_vector")
        ones_made = sem("ones_made")
        z_ready = sem("z_ready")
        z_used = sem("z_used")
        scaled = [None, sem("scaled1"), sem("scaled2")]
        biased = [sem(f"biased{k}") for k in range(3)]
        squared = [sem(f"squared{k}") for k in range(3)]
        summed = [sem(f"summed{k}") for k in range(3)]
        norm_done = sem("norm_done")
        root_done = sem("root_done")
        r_step = sem("r_step")
        h_ready = sem("h_ready")
        h1_ps = sem("h1_ps")
        h1_done = sem("h1_done")
        h2_ps = sem("h2_ps")
        h2_done = sem("h2_done")
        y_ps = sem("y_ps")
        y_done = sem("y_done")
        y_stored = sem("y_stored")

        PARTS = [slice(0, BATCH - CB), slice(BATCH - CB, BATCH)]
        PAIR_LOADS = 2 * PER_TILE + 1
        R_STEPS = 4

        def group_no(body, i):
            return body * PER_BODY + (NP + i)

        def groups_through(k, chunk):
            if k == 1:
                return group_no(chunk, NG)
            if k == 0:
                return NP if isinstance(chunk, int) and chunk == 0 else group_no(chunk - 1, NG + NP)
            return group_no(chunk, PER_BODY) - (NP if isinstance(chunk, int) and chunk == CHUNKS - 1 else 0)

        def splits_of(i):
            return [n for n, m in enumerate(SPLIT_FIELDS) if m // GROUP == i]

        def part_slot(k, n):
            return ((k - 1) * SPLIT + n) % SPLIT_SLOTS

        def split_slot_free(c, k, n):
            before = (k - 1) * SPLIT + n - SPLIT_SLOTS
            if before < 0:
                if isinstance(c, int) and c == 0:
                    return None
                c = c - 1
            k, n = SPLIT_SEQ[before]
            return group_no(c, group_at(c, k, SPLIT_FIELDS[n] // GROUP)) + 1

        def low_no(c, k, n):
            same = [m for m in range(SPLIT) if LOW_ON_VECTOR[m] == LOW_ON_VECTOR[n]]
            return c * (2 * len(same)) + (k - 1) * len(same) + same.index(n)

        def split_no(c, k, n):
            return c * (2 * SPLIT) + (k - 1) * SPLIT + n

        def low_part(eng, engine, c, k, n, done):
            m = SPLIT_FIELDS[n]
            slot = (NP + group_at(c, k, m // GROUP)) % RING
            eng.wait_ge(hi_ready, split_no(c, k, n) + 1)
            engine.tensor_tensor(out=z_lo[:, part_slot(k, n), :], in0=z[:, slot, m % GROUP, :],
                                 in1=z_hi[:, part_slot(k, n), :].bitcast(f32), op=ALU.subtract).then_inc(done, 1)

        def group_at(c, k, i):
            return i if k == 1 else NG + i + (0 if isinstance(c, int) and c == CHUNKS - 1 else NP)

        def over_bodies(eng, body):
            body(0, True, False)
            with eng.Fori(1, CHUNKS - 1) as c:
                body(c, False, False)
            body(CHUNKS - 1, False, True)

        block = ctx.enter_context(nc.Block())

        @block.gpsimd
        def _(pool):
            nc.gpsimd.memset(ones[:, :], 1.0).then_inc(ones_made, 1)

            def make_rows(c, parity):
                nc.gpsimd.tensor_tensor(out=idx[:, parity, :], in0=ids_sb[:, bass.ds(c * GATHERS, GATHERS)],
                                        in1=base_sb[:, :], op=ALU.add).then_inc(idx_made, 1)

            def start_chunk(c, parity, last=False):
                if not (isinstance(c, int) and c < 1):
                    pool.wait_ge(gather_done, c * (16 * GATHERS))
                if not (isinstance(c, int) and c < 2):
                    pool.wait_ge(scratch_written, (c - 1) * 48)
                pool.wait_ge(idx_made, c + 1)
                if not last:
                    make_rows(c + 1, 1 - parity)

            def gather(parity, j):
                n = 128 if j < GATHERS - 1 else LAST_SLOTS
                nc.gpsimd.indirect_dma_start(
                    out=gathered[0:n, parity, j, :], out_offset=None, in_=table[:, :],
                    in_offset=bass.IndirectOffsetOnAxis(ap=idx[0:n, parity, j:j + 1], axis=0)
                ).then_inc(gather_done, 16)

            def body(c, parity, more=True, last=False):
                if more:
                    start_chunk(c + 2, parity, last)
                lows = [(k, n) for k, n in SPLIT_SEQ if not LOW_ON_VECTOR[n]]
                every = len(lows) // GATHERS
                for at, (k, n) in enumerate(lows):
                    low_part(pool, nc.gpsimd, c, k, n, lo_ready_pool)
                    if more and at % every == 0 and at // every < GATHERS:
                        gather(parity, at // every)

            pool.wait_ge(ids_loaded, 32)
            make_rows(0, 0)
            for c in range(2):
                start_chunk(c, c)
                for j in range(GATHERS):
                    gather(c, j)
            body(0, 0)
            with pool.Fori(1, CHUNKS - 4, 2) as c:
                body(c, 1)
                body(c + 1, 0)
            body(CHUNKS - 3, 1, True, True)
            body(CHUNKS - 2, 0, False)
            body(CHUNKS - 1, 1, False)

        @block.sync
        def _(sp):
            def store_chunk(c, parity):
                g = gathered[:, parity, :, :]
                dst = scratch[bass.ds(c, 1), :, :].rearrange("c n e -> (c n) e")
                full = (GATHERS - 1) * 128
                sp.dma_start(dst[0:full, :].rearrange("(j p) e -> p j e", p=128),
                             g[:, 0:GATHERS - 1, :]).then_inc(scratch_written, 16)
                sp.dma_start(dst[full:full + LAST_SLOTS, :].rearrange("(j p) e -> p j e", p=LAST_SLOTS),
                             g[0:LAST_SLOTS, GATHERS - 1:GATHERS, :]).then_inc(scratch_written, 16)
                sp.dma_start(dst[FIELDS * CB:SCRATCH_FIELDS * CB, :].rearrange("(j p) e -> p j e", p=128),
                             g[:, 0:5, :]).then_inc(scratch_written, 16)

            def chunk_rows(c):
                return scratch[bass.ds(c, 1), :, :].rearrange("c (m b) e -> (c m) (b e)", b=CB)

            def load_pairs(c):
                rows = chunk_rows(c)
                for kk in range(PER_TILE):
                    at = slice(kk * FIELDS, (kk + 1) * FIELDS)
                    sp.dma_start(x_rep[at, :], rows[0:FIELDS, :]).then_inc(pairs_loaded, 16)
                    tiles = [PAIR_TILES, PAIR_TILES - 1, PAIR_TILES - 1][kk]
                    first = rows[1 + kk:1 + kk + FIELDS, :]
                    window = bass.AP(first.tensor, first.offset,
                                     [[ROWS, FIELDS], [PER_TILE * ROWS, tiles], [1, ROWS]])
                    sp.dma_start(x_rot[at, 0:tiles, :], window).then_inc(pairs_loaded, 16)
                sp.dma_start(x_rot[FIELDS:2 * FIELDS, PAIR_TILES - 1, :],
                             rows[0:FIELDS, :]).then_inc(pairs_loaded, 16)

            def load_fields(c, g):
                rows = chunk_rows(c)[g * GROUP:(g + 1) * GROUP, :].rearrange("m n -> (m n)")
                sp.dma_start(x_all[:, g * GROUP:(g + 1) * GROUP, :].rearrange("p m n -> p (m n)"),
                             rows.partition_broadcast(128)).then_inc(fields_loaded[g], 16)

            sp.dma_start(ids_sb[:, :], idx_in).then_inc(ids_loaded, 16)
            sp.dma_start(base_sb[:, :], base_in).then_inc(ids_loaded, 16)
            sp.wait_ge(gather_done, 16 * GATHERS)
            store_chunk(0, 0)
            sp.wait_ge(scratch_written, 48)
            load_pairs(0)
            for g in range(NG):
                if g == (FIELDS - 2 * STAGE_TILES) // GROUP:
                    sp.wait_ge(w_lo_made, 2)
                load_fields(0, g)
            sp.wait_ge(gather_done, 2 * 16 * GATHERS)
            store_chunk(1, 1)

            def next_chunk(c, more, parity=0):
                sp.wait_ge(scratch_written, (c + 2) * 48)
                sp.wait_ge(z_ready, c * PER_BODY + (NP if isinstance(c, int) and c == 0 else NP - NG))
                load_pairs(c + 1)
                for g in range(NG):
                    sp.wait_ge(z_ready, group_no(c, NG + NP + g + 1))
                    load_fields(c + 1, g)
                if more:
                    sp.wait_ge(gather_done, (c + 3) * (16 * GATHERS))
                    store_chunk(c + 2, parity)

            next_chunk(0, True)
            with sp.Fori(1, CHUNKS - 3, 2) as c:
                next_chunk(c, True, 1)
                next_chunk(c + 1, True, 0)
            next_chunk(CHUNKS - 3, True, 1)
            next_chunk(CHUNKS - 2, False)
            sp.wait_ge(z_ready, group_no(CHUNKS - 1, NG + 5))
            sp.dma_start(top1_sb, w_top1[0:3 * 128, :].rearrange("(k p) n -> p k n", p=128)).then_inc(top_loaded, 16)
            sp.dma_start(top1c_sb, w_top1[3 * 128:3 * 128 + EMB, :]).then_inc(top_loaded, 16)
            sp.dma_start(ctx_sb, ctx_t).then_inc(top_loaded, 16)
            sp.dma_start(top2_sb, w_top2.rearrange("(k p) n -> p k n", p=128)).then_inc(top_loaded, 16)
            sp.wait_ge(y_done, 1)
            sp.dma_start(out, y_sb[:, :]).then_inc(y_stored, 16)
            sp.wait_ge(y_stored, 16)

        @block.scalar
        def _(act):
            act.dma_start(w0_sb[0:PAIR_ROWS, :, :], w0a).then_inc(w0_loaded, 16)
            act.dma_start(w0b_sb[0:PAIR_ROWS, 0:PAIR_TILES, :], w0b).then_inc(w0_loaded, 16)
            for k, b in enumerate((b0, b1, b2)):
                act.dma_start(bias[:, k:k + 1], b).then_inc(bias_loaded, 16)

            for k, w in ((1, w1), (2, w2)):
                act.dma_start(w_raw[k], w[:, 0:SPLIT, :]).then_inc(w_split_loaded[k], 16)
            act.dma_start(w_sb[1][:, :, :], w1[:, SPLIT:FIELDS, :]).then_inc(w_loaded[1], 16)
            for k in (1, 2):
                act.wait_ge(w_split_loaded[k], 16)
                nc.scalar.activation(w_hi[k][:, :, :], w_raw[k], ACT.Copy).then_inc(w_hi_made, 1)
            act.wait_ge(pairs_loaded, PAIR_LOADS * 16)
            act.dma_start(w_sb[2][:, :, :], w2[:, SPLIT:FIELDS, :]).then_inc(w_loaded[2], 16)
            act.dma_start(top3_sb[:, :], w_top3).then_inc(top_bias_loaded, 16)
            act.dma_start(btop1_sb[:, :], b_top1).then_inc(top_bias_loaded, 16)
            act.dma_start(btop2_sb[:, :], b_top2).then_inc(top_bias_loaded, 16)
            act.wait_ge(bias_loaded, 48)

            def finish(k, c):
                if k == 0:
                    act.wait_ge(z_used, groups_through(0, c))
                    src = acc[0][:, :]
                else:
                    act.wait_ge(scaled[k], c + 1)
                    src = u[k][:, :]
                nc.scalar.activation(t[k], src, ACT.Identity, bias=bias[:, k:k + 1]).then_inc(biased[k], 1)
                if k == 0 and not (isinstance(c, int) and c == 0):
                    act.wait_ge(summed[0], c)
                nc.scalar.activation(u[k][:, :], src, ACT.Square, bias=bias[:, k:k + 1]).then_inc(squared[k], 1)

            def roots(n, ks):
                act.wait_ge(norm_done, n + 1)
                if not (isinstance(n, int) and n == 0):
                    act.wait_ge(r_step, n * R_STEPS)
                nc.scalar.activation(root[:, ks[0]:ks[-1] + 1, :],
                                     norm2[:, ks[0] * CB:(ks[-1] + 1) * CB].rearrange("p (k b) -> p k b", b=CB),
                                     ACT.Sqrt).then_inc(root_done, 1)

            def highs(c, k, i):
                for n in splits_of(i):
                    free = split_slot_free(c, k, n)
                    if free is not None:
                        act.wait_ge(z_used, free)
                    act.wait_ge(z_ready, group_no(c, group_at(c, k, i)) + 1)
                    slot = (NP + group_at(c, k, i)) % RING
                    nc.scalar.activation(z_hi[:, part_slot(k, n), :], z[:, slot, SPLIT_FIELDS[n] % GROUP, :],
                                         ACT.Copy).then_inc(hi_ready, 1)

            def body(c, first, last):
                for i in range(NG):
                    highs(c, 1, i)
                    if i == 3 and not first:
                        finish(2, c - 1)
                finish(1, c)
                for i in range(NG):
                    highs(c, 2, i)
                    if i == 1 and not last:
                        finish(0, c + 1)
                    if i == 8:
                        roots(c + 1, [k for k in range(3) if not (k == 0 and last) and not (k == 2 and first)])

            finish(0, 0)
            roots(0, [0])
            over_bodies(act, body)
            finish(2, CHUNKS - 1)
            roots(CHUNKS + 1, [2])


            act.wait_ge(top_bias_loaded, 3 * 16)

            def relu1(part):
                for n in range(TOP1 // 128):
                    act.wait_ge(h1_ps, part * (TOP1 // 128) + n + 1)
                    nc.scalar.activation(h1[:, n, PARTS[part]], top_ps[n][:, PARTS[part]], ACT.Relu,
                                         bias=btop1_sb[:, n:n + 1]).then_inc(h1_done, 1)

            def relu2(part):
                for n in range(TOP2 // 128):
                    act.wait_ge(h2_ps, part * (TOP2 // 128) + n + 1)
                    nc.scalar.activation(h2[:, n, PARTS[part]], acc[n][:, PARTS[part]], ACT.Relu,
                                         bias=btop2_sb[:, n:n + 1]).then_inc(h2_done, 1)

            relu1(0)
            relu1(1)
            relu2(0)
            relu2(1)
            act.wait_ge(y_ps, 1)
            nc.scalar.copy(y_sb[:, :], acc[2][0:1, :]).then_inc(y_done, 1)

        @block.tensor
        def _(pe):
            def use_group(c, i, k, tiles, chunk):
                g = group_no(c, i)
                slot = (NP + i) % RING
                total = PAIR_TILES if k == 0 else FIELDS
                if tiles[0] == 0 and not (isinstance(chunk, int) and chunk == 0):
                    pe.wait_ge(squared[0] if k == 0 else scaled[k], chunk)
                pe.wait_ge(z_ready, g + 1)
                splits = splits_of(tiles[0] // GROUP) if k else []
                for j, tile in enumerate(tiles[:len(tiles) - len(splits)]):
                    rows = 128 if k else (LAST_PAIR_ROWS if tile == PAIR_TILES - 1 else PAIR_ROWS)
                    w = w_sb[k][:, WHOLE_FIELDS.index(tile), :] if k else w0_sb[0:rows, tile, :]
                    mm = nc.tensor.matmul(acc[k][:, :], w, z[0:rows, slot, j, :],
                                          start=(tile == 0), stop=(tile == total - 1))
                for n in splits:
                    pe.wait_ge(lo_ready_vector if LOW_ON_VECTOR[n] else lo_ready_pool, low_no(c, k, n) + 1)
                    for w, x in ((w_lo, z_hi), (w_hi, z_hi), (w_hi, z_lo)):
                        mm = nc.tensor.matmul(acc[k][:, :], w[k][:, n, :], x[:, part_slot(k, n), :],
                                              start=False, stop=(x is z_lo and SPLIT_FIELDS[n] == FIELDS - 1))
                mm.then_inc(z_used, 1)

            def norms(n, ks, chunks):
                for k, ch in zip(ks, chunks):
                    pe.wait_ge(summed[k], ch + 1)
                if not (isinstance(n, int) and n == 0):
                    pe.wait_ge(r_step, n * R_STEPS)
                nc.tensor.matmul(norm2[:, ks[0] * CB:(ks[-1] + 1) * CB], ones[:, :],
                                 ssq[:, ks[0]:ks[-1] + 1, :].rearrange("p k b -> p (k b)"),
                                 start=True, stop=True).then_inc(norm_done, 1)

            def body(c, first, last):
                if first:
                    pe.wait_ge(w_loaded[1], 16)
                    pe.wait_ge(w_lo_made, 1)
                for i, tiles in enumerate(CIN_GROUPS):
                    use_group(c, i, 1, tiles, c)
                if not last:
                    for i, tiles in enumerate(PAIR_GROUPS):
                        use_group(c, NG + i, 0, tiles, c + 1)
                skip = NP if last else 0
                if first:
                    pe.wait_ge(w_loaded[2], 16)
                    pe.wait_ge(w_lo_made, 2)
                for i, tiles in enumerate(CIN_GROUPS):
                    use_group(c, NG + NP - skip + i, 2, tiles, c)
                    if i == 5:
                        ks = [k for k in range(3) if not (k == 0 and last) and not (k == 2 and first)]
                        norms(c + 1, ks, [c + 1 - k for k in ks])

            pe.wait_ge(w0_folded, 2)
            pe.wait_ge(ones_made, 1)
            for i, tiles in enumerate(PAIR_GROUPS):
                use_group(0, i - NP, 0, tiles, 0)
            norms(0, [0], [0])
            over_bodies(pe, body)

            pe.wait_ge(top_loaded, 4 * 16)
            pe.wait_ge(top_bias_loaded, 3 * 16)
            N1, N2 = TOP1 // 128, TOP2 // 128
            feats = [(top1c_sb, ctx_sb)] + \
                    [(top1_sb[:, k, :], h0[:, k * BATCH:(k + 1) * BATCH]) for k in range(3)]

            def top1(part, k):
                w, x = feats[k]
                for n in range(N1):
                    if part and k == 0:
                        pe.wait_ge(h1_done, n + 1)
                    mm = nc.tensor.matmul(top_ps[n][:, PARTS[part]], w[:, n * 128:(n + 1) * 128],
                                          x[:, PARTS[part]], start=(k == 0), stop=(k == 3))
                    if k == 3:
                        mm.then_inc(h1_ps, 1)

            def top2(part):
                for k in range(N1):
                    pe.wait_ge(h1_done, part * N1 + k + 1)
                    if part and k == 0:
                        pe.wait_ge(h2_done, N2)
                    for n in range(N2):
                        mm = nc.tensor.matmul(acc[n][:, PARTS[part]], top2_sb[:, k, n * 128:(n + 1) * 128],
                                              h1[:, k, PARTS[part]], start=(k == 0), stop=(k == N1 - 1))
                        if k == N1 - 1:
                            mm.then_inc(h2_ps, 1)

            def top3(part):
                for k in range(N2):
                    pe.wait_ge(h2_done, part * N2 + k + 1)
                    mm = nc.tensor.matmul(acc[2][0:1, PARTS[part]], top3_sb[:, k:k + 1], h2[:, k, PARTS[part]],
                                          start=(k == 0), stop=(k == N2 - 1))
                return mm

            pe.wait_ge(h_ready, CHUNKS + 1)
            for k in range(2):
                top1(0, k)
            norms(CHUNKS + 1, [2], [CHUNKS - 1])
            for k in range(2, 4):
                top1(0, k)
            pe.wait_ge(h_ready, CHUNKS + 2)
            for k in range(4):
                top1(1, k)
            top2(0)
            top2(1)
            top3(0)
            top3(1).then_inc(y_ps, 1)

        @block.vector
        def _(dve):
            def make_group(c, i, k, tiles, chunk):
                g = group_no(c, i)
                slot = (NP + i) % RING
                n = len(tiles)
                if not (isinstance(g, int) and g < RING):
                    dve.wait_ge(z_used, g + 1 - RING)
                if k == 0:
                    if tiles[0] == 0:
                        dve.wait_ge(pairs_loaded, (chunk + 1) * (PAIR_LOADS * 16))
                    rows = LAST_PAIR_ROWS if tiles[-1] == PAIR_TILES - 1 else PAIR_ROWS
                    a = x_rep[0:rows, :]
                    b = x_rot[0:rows, tiles[0]:tiles[0] + n, :]
                else:
                    if k == 1:
                        dve.wait_ge(fields_loaded[i], (chunk + 1) * 16)
                    if tiles[0] == 0:
                        dve.wait_ge(biased[k - 1], chunk + 1)
                    rows = 128
                    a = t[k - 1]
                    b = x_all[:, tiles[0]:tiles[0] + n, :]
                nc.vector.tensor_tensor(out=z[0:rows, slot, 0:n, :], in0=a.unsqueeze(1).to_broadcast([rows, n, ROWS]),
                                        in1=b, op=ALU.mult).then_inc(z_ready, 1)

            def weights_low(k):
                dve.wait_ge(w_hi_made, k)
                nc.vector.tensor_tensor(out=w_lo[k][:, :, :], in0=w_raw[k], in1=w_hi[k][:, :, :].bitcast(f32),
                                        op=ALU.subtract).then_inc(w_lo_made, 1)

            def lows(c, k, i):
                for n in splits_of(i):
                    if LOW_ON_VECTOR[n]:
                        low_part(dve, nc.vector, c, k, n, lo_ready_vector)

            def scale(k, c, n):
                dve.wait_ge(z_used, groups_through(k, c))
                dve.wait_ge(r_step, n * R_STEPS)
                nc.vector.tensor_tensor(
                    out=u[k][:, :].rearrange("p (b e) -> p b e", e=EMB),
                    in0=acc[k][:, :].rearrange("p (b e) -> p b e", e=EMB),
                    in1=r[:, k - 1, :].unsqueeze(2).to_broadcast([128, CB, EMB]), op=ALU.mult).then_inc(scaled[k], 1)

            def sums(k, c):
                dve.wait_ge(biased[k], c + 1)
                nc.vector.tensor_reduce(dsum[:, k, :], t[k].rearrange("p (b e) -> p b e", e=EMB), AX.X, ALU.add)
                dve.wait_ge(squared[k], c + 1)
                nc.vector.tensor_reduce(ssq[:, k, :], u[k][:, :].rearrange("p (b e) -> p b e", e=EMB),
                                        AX.X, ALU.add).then_inc(summed[k], 1)

            def reciprocals(n, ks):
                s = slice(ks[0], ks[-1] + 1)
                sq = norm2[:, ks[0] * CB:(ks[-1] + 1) * CB].rearrange("p (k b) -> p k b", b=CB)
                dve.wait_ge(root_done, n + 1)
                nc.vector.reciprocal(ra[:, s, :], root[:, s, :]).then_inc(r_step, 1)
                dve.wait_ge(r_step, n * R_STEPS + 1)
                nc.vector.scalar_tensor_tensor(out=rb[:, s, :], in0=sq, scalar=F32_MAX, in1=ra[:, s, :],
                                               op0=ALU.min, op1=ALU.mult).then_inc(r_step, 1)
                dve.wait_ge(r_step, n * R_STEPS + 2)
                nc.vector.scalar_tensor_tensor(out=rc[:, s, :], in0=rb[:, s, :], scalar=-0.5, in1=ra[:, s, :],
                                               op0=ALU.mult, op1=ALU.mult).then_inc(r_step, 1)
                dve.wait_ge(r_step, n * R_STEPS + 3)
                nc.vector.scalar_tensor_tensor(out=r[:, s, :], in0=rc[:, s, :], scalar=1.5, in1=ra[:, s, :],
                                               op0=ALU.add, op1=ALU.mult).then_inc(r_step, 1)
                dve.wait_ge(r_step, n * R_STEPS + 4)
                k0 = ks[0]
                feats = h0[:, bass.ds(n * CB + k0 * (BATCH - CB), (len(ks) - 1) * (BATCH - CB) + CB)]
                feats = bass.AP(feats.tensor, feats.offset, [feats.ap[0], [BATCH - CB, len(ks)], [1, CB]])
                nc.vector.tensor_tensor(out=feats, in0=r[:, s, :], in1=dsum[:, s, :], op=ALU.mult).then_inc(h_ready, 1)

            def body(c, first, last):
                for i, tiles in enumerate(CIN_GROUPS):
                    make_group(c, i, 1, tiles, c)
                    lows(c, 1, i - 1)
                    if i == 3 and not first:
                        scale(2, c - 1, c + 1)
                    if i == 6 and not first:
                        sums(2, c - 1)
                lows(c, 1, NG - 1)
                if not last:
                    for i, tiles in enumerate(PAIR_GROUPS):
                        make_group(c, NG + i, 0, tiles, c + 1)
                skip = NP if last else 0
                scale(1, c, c + 1)
                ks = [k for k in range(3) if not (k == 0 and last) and not (k == 2 and first)]
                for i, tiles in enumerate(CIN_GROUPS):
                    make_group(c, NG + NP - skip + i, 2, tiles, c)
                    lows(c, 2, i - 1)
                    if i == 1:
                        sums(1, c)
                    if i == 3 and not last:
                        sums(0, c + 1)
                    if i == 10:
                        reciprocals(c + 1, ks)
                lows(c, 2, NG - 1)

            dve.wait_ge(w0_loaded, 32)
            full = slice(0, PAIR_TILES - 1)
            nc.vector.tensor_tensor(out=w0_sb[0:PAIR_ROWS, full, :], in0=w0_sb[0:PAIR_ROWS, full, :],
                                    in1=w0b_sb[0:PAIR_ROWS, full, :], op=ALU.add).then_inc(w0_folded, 1)
            nc.vector.tensor_tensor(out=w0_sb[0:FIELDS, PAIR_TILES - 1, :], in0=w0_sb[0:FIELDS, PAIR_TILES - 1, :],
                                    in1=w0b_sb[0:FIELDS, PAIR_TILES - 1, :], op=ALU.add).then_inc(w0_folded, 1)
            dve.wait_ge(w0_folded, 2)
            weights_low(1)
            weights_low(2)
            for i, tiles in enumerate(PAIR_GROUPS):
                make_group(0, i - NP, 0, tiles, 0)
            sums(0, 0)
            reciprocals(0, [0])
            over_bodies(dve, body)
            scale(2, CHUNKS - 1, CHUNKS + 1)
            sums(2, CHUNKS - 1)
            reciprocals(CHUNKS + 1, [2])


def kernel(**inputs):
    import concourse.bacc as bacc
    from concourse.bass_utils import run_bass_kernel_spmd

    def lay(a):
        return np.ascontiguousarray(a)

    tables = [np.asarray(inputs[f"tbl_{f}"]) for f in range(FIELDS)]
    starts = np.concatenate([[0], np.cumsum([a.shape[0] for a in tables])])[:FIELDS].astype(np.int32)
    slot_fields = GATHERS * SLOT_FIELDS

    def slots(a):
        a = a.reshape(CHUNKS, CB, FIELDS).transpose(0, 2, 1)
        a = np.concatenate([a, np.zeros((CHUNKS, slot_fields - FIELDS, CB), a.dtype)], axis=1)
        a = a.reshape(CHUNKS, GATHERS, SLOT_FIELDS * CB)
        return lay(a.transpose(2, 0, 1).reshape(128, CHUNKS * GATHERS))

    order_a = np.zeros((PAIR_ROWS, PAIR_TILES), np.int64)
    order_b = np.zeros((PAIR_ROWS, PAIR_TILES), np.int64)
    for n, k in enumerate(PAIR_OFFSETS):
        for i in range(FIELDS):
            j = (i + k) % FIELDS
            at = (n % PER_TILE * FIELDS + i, n // PER_TILE)
            order_a[at], order_b[at] = i * FIELDS + j, j * FIELDS + i
    w0 = np.asarray(inputs["L0_rec_w0"])

    def fields_first(w):
        return lay(w.reshape(FIELDS, UNITS, UNITS).transpose(1, 0, 2)[:, WEIGHT_ORDER, :])

    arrays = {
        "ids": slots(np.asarray(inputs["ids"])),
        "bases": lay(slots(np.broadcast_to(starts, (BATCH, FIELDS)))[:, 0:GATHERS]),
        "table": lay(np.concatenate(tables, axis=0)),
        "ctx_t": lay(np.asarray(inputs["dense_ctx"]).T),
        "w0a": lay(w0[order_a]),
        "w0b": lay(w0[order_b]),
        "w1": fields_first(np.asarray(inputs["L0_rec_w1"])),
        "w2": fields_first(np.asarray(inputs["L0_rec_w2"])),
        "b0": lay(np.asarray(inputs["L0_rec_b0"]).reshape(UNITS, 1)),
        "b1": lay(np.asarray(inputs["L0_rec_b1"]).reshape(UNITS, 1)),
        "b2": lay(np.asarray(inputs["L0_rec_b2"]).reshape(UNITS, 1)),
        "w_top1": lay(inputs["W_top1"]),
        "b_top1": lay(np.asarray(inputs["b_top1"]).reshape(TOP1 // 128, 128).T),
        "w_top2": lay(inputs["W_top2"]),
        "b_top2": lay(np.asarray(inputs["b_top2"]).reshape(TOP2 // 128, 128).T),
        "w_top3": lay(np.asarray(inputs["W_top3"]).reshape(TOP2 // 128, 128).T),
    }
    nc = bacc.Bacc("TRN2", target_bir_lowering=False, num_devices=1, dynamic_dma_scratch_size=DMA_SCRATCH)
    args = [nc.dram_tensor(f"in_{name}", a.shape, mybir.dt.from_np(a.dtype), kind="ExternalInput").ap()
            for name, a in arrays.items()]
    args.append(nc.dram_tensor("scores", (1, BATCH), mybir.dt.float32, kind="ExternalOutput").ap())
    cin_kernel(nc, *args)
    got = run_bass_kernel_spmd(nc, [{f"in_{name}": a for name, a in arrays.items()}], core_ids=[0])
    return got.results[0]["scores"].reshape(BATCH, 1)
```

```python
import concourse.bass as bass
import numpy as np
from concourse import mybir
from contextlib import ExitStack

FIELDS = 39
EMB = 16
BATCH = 512
UNITS = 128
TOP1, TOP2 = 512, 256
CB = 32
CHUNKS = BATCH // CB
ROWS = CB * EMB
GATHERS = 10
SLOT_FIELDS = 128 // CB
LAST_SLOTS = FIELDS * CB - (GATHERS - 1) * 128

OFFSETS = (FIELDS + 1) // 2
PER_TILE = 128 // FIELDS
PAIR_TILES = -(-OFFSETS // PER_TILE)
PAIR_ROWS = PER_TILE * FIELDS
LAST_PAIR_ROWS = (OFFSETS - PER_TILE * (PAIR_TILES - 1)) * FIELDS
PAIR_OFFSETS = list(range(1, OFFSETS)) + [0]

GROUP = 3
CIN_GROUPS = [list(range(g, g + GROUP)) for g in range(0, FIELDS, GROUP)]
PAIR_GROUPS = [[0, 1], [2, 3], [4, 5], [6]]
NG, NP = len(CIN_GROUPS), len(PAIR_GROUPS)
ORDER = [(1, i) for i in range(NG)] + [(0, i) for i in range(NP)] + [(2, i) for i in range(NG)]
LAST_ORDER = [(k, i) for k, i in ORDER if k]
PER_BODY = len(ORDER)
RING = 5

SPLITS_IN_GROUP = [2, 1, 2, 2, 2, 2, 2, 2, 2, 2, 2, 2, 1]
SPLIT_FIELDS = [GROUP * (g + 1) - 1 - n for g in range(NG) for n in reversed(range(SPLITS_IN_GROUP[g]))]
WHOLE_FIELDS = [m for m in range(FIELDS) if m not in SPLIT_FIELDS]
WEIGHT_ORDER = SPLIT_FIELDS + WHOLE_FIELDS
SPLIT = len(SPLIT_FIELDS)
SPLIT_SLOTS = 6
DMA_SCRATCH = 4096
SPLIT_SEQ = [(k, n) for k in (1, 2) for n in range(SPLIT)]
LOW_ON_VECTOR = [n % 5 == 4 for n in range(SPLIT)]
GATHERS_IN_LAYER0 = 7
GATHER_EVERY = 8
STAGE_TILES = -(-SPLIT * UNITS // ROWS)
assert PER_BODY % RING == 0 and FIELDS % GROUP == 0
SCRATCH_FIELDS = FIELDS + 5 * SLOT_FIELDS


def cin_kernel(nc, idx_in, base_in, table, ctx_t, w0a, w0b, w1, w2, b0, b1, b2,
               w_top1, b_top1, w_top2, b_top2, w_top3, out):
    f32, f32r, i32 = mybir.dt.float32, mybir.dt.float32r, mybir.dt.int32
    ALU, ACT, AX = mybir.AluOpType, mybir.ActivationFunctionType, mybir.AxisListType
    F32_MAX = float(np.finfo(np.float32).max)

    features = nc.dram_tensor("h_scratch", [128, 3 * BATCH], f32, kind="Internal").ap()
    scratch = nc.dram_tensor("x_scratch", [CHUNKS, SCRATCH_FIELDS * CB, EMB], f32, kind="Internal").ap()

    with ExitStack() as ctx:
        def sb(name, shape, dt=f32):
            return ctx.enter_context(nc.sbuf_tensor(name, shape, dt))

        def pb(name):
            return ctx.enter_context(nc.psum_tensor(name, [128, 512], f32))

        def sem(name):
            return ctx.enter_context(nc.semaphore(name))

        ids_sb = sb("ids_sb", [128, CHUNKS * GATHERS], i32)
        base_sb = sb("base_sb", [128, GATHERS], i32)
        idx = sb("idx", [128, 2, GATHERS], i32)
        gathered = sb("gathered", [128, 2, GATHERS, EMB])
        x_pairs = sb("x_pairs", [128, PAIR_TILES + 1, ROWS])
        x_rot = x_pairs[:, 0:PAIR_TILES, :]
        x_rep = x_pairs[:, PAIR_TILES, :]
        x_all = sb("x_all", [128, FIELDS, ROWS])
        z = sb("z", [128, RING, GROUP, ROWS])
        ssq = sb("ssq", [128, 3, CB])
        dsum = sb("dsum", [128, 3, CB])
        root = sb("root", [128, 3, CB])
        r = sb("r", [128, 3, CB])
        ones = sb("ones", [128, 128])
        w0_sb = sb("w0_sb", [128, PAIR_TILES, UNITS])
        w_sb = {k: sb(f"w{k}_sb", [128, len(WHOLE_FIELDS), UNITS]) for k in (1, 2)}
        w_hi = {k: sb(f"w{k}_hi", [128, SPLIT, UNITS], f32r) for k in (1, 2)}
        w_lo = {k: sb(f"w{k}_lo", [128, SPLIT, UNITS], f32r) for k in (1, 2)}
        z_hi = sb("z_hi", [128, SPLIT_SLOTS, ROWS], f32r)
        z_lo = sb("z_lo", [128, SPLIT_SLOTS, ROWS], f32r)
        bias = sb("bias", [128, 3])
        top3_sb = sb("top3_sb", [128, TOP2 // 128])
        btop1_sb = sb("btop1_sb", [128, TOP1 // 128])
        btop2_sb = sb("btop2_sb", [128, TOP2 // 128])
        z_tiles = z[:, :, :, :].rearrange("p s j n -> p (s j) n")
        w0b_sb = z_tiles[:, RING * GROUP - 2:RING * GROUP, :].rearrange("p a (b o) -> p (a b) o", o=UNITS)
        w_raw = {k: x_all[:, FIELDS - k * STAGE_TILES:FIELDS - (k - 1) * STAGE_TILES, :]
                 .rearrange("p a (b o) -> p (a b) o", o=UNITS)[:, 0:SPLIT, :] for k in (1, 2)}
        h1 = x_all[:, 0:TOP1 // 128, :]
        h2 = x_all[:, TOP1 // 128:TOP1 // 128 + TOP2 // 128, :]
        y_sb = x_all[0:1, 6, :]
        top1_sb = x_pairs[:, 0:3, :]
        top1c_sb = x_pairs[0:EMB, 3, :]
        ctx_sb = x_pairs[0:EMB, 4, :]
        top2_sb = x_all[:, 7:9, :].rearrange("p a (b n) -> p (a b) n", n=TOP2)

        h0 = x_pairs[:, PAIR_TILES - 2:PAIR_TILES + 1, :].rearrange("p k n -> p (k n)")

        acc = [pb("acc0"), pb("acc1"), pb("acc2")]
        norm2 = pb("norm2")
        top_ps = [pb(f"top{n}") for n in range(TOP1 // 128)]
        u = [top_ps[0], top_ps[1], norm2]
        t = [top_ps[2][:, :], top_ps[3][:, :], norm2[:, :]]

        ids_loaded = sem("ids_loaded")
        idx_made = sem("idx_made")
        gather_done = sem("gather_done")
        scratch_written = sem("scratch_written")
        pairs_loaded = [sem(f"pairs_loaded{p}") for p in range(NP)]
        fields_loaded = [sem(f"fields_loaded{g}") for g in range(NG)]
        w0_loaded = sem("w0_loaded")
        w0_folded = sem("w0_folded")
        bias_loaded = sem("bias_loaded")
        w_loaded = {1: sem("w1_loaded"), 2: sem("w2_loaded")}
        top_loaded = sem("top_loaded")
        top2_loaded = sem("top2_loaded")
        top_bias_loaded = sem("top_bias_loaded")
        w_split_loaded = {k: sem(f"w{k}_split_loaded") for k in (1, 2)}
        w_hi_made = sem("w_hi_made")
        w_lo_made = sem("w_lo_made")
        hi_ready = sem("hi_ready")
        lo_ready_pool = sem("lo_ready_pool")
        lo_ready_vector = sem("lo_ready_vector")
        ones_made = sem("ones_made")
        z_ready = sem("z_ready")
        z_used = sem("z_used")
        scaled = [None, sem("scaled1"), sem("scaled2")]
        biased = [sem(f"biased{k}") for k in range(3)]
        squared = [sem(f"squared{k}") for k in range(3)]
        values_summed = sem("values_summed")
        summed = [sem(f"summed{k}") for k in range(3)]
        norm_done = sem("norm_done")
        root_done = sem("root_done")
        r_step = sem("r_step")
        h_ready = sem("h_ready")
        h_stored = sem("h_stored")
        h_loaded = sem("h_loaded")
        h1_ps = sem("h1_ps")
        h1_done = sem("h1_done")
        h2_ps = sem("h2_ps")
        h2_done = sem("h2_done")
        y_ps = sem("y_ps")
        y_done = sem("y_done")
        y_stored = sem("y_stored")

        PAIR_LOADS = [sum(PER_TILE * g[0] + kk < OFFSETS for kk in range(PER_TILE)) + (PER_TILE if g[0] == 0 else 0)
                      for g in PAIR_GROUPS]
        R_STEPS = 4

        def group_no(body, i):
            return body * PER_BODY + (NP + i)

        def order_of(body):
            return LAST_ORDER if isinstance(body, int) and body == CHUNKS - 1 else ORDER

        def group_at(body, k, i):
            return order_of(body).index((k, i))

        def groups_through(k, chunk):
            if k == 0:
                return NP if isinstance(chunk, int) and chunk == 0 else \
                    group_no(chunk - 1, group_at(0, 0, NP - 1) + 1)
            return group_no(chunk, group_at(chunk, k, (NG if k else NP) - 1) + 1)

        def splits_of(i):
            return [n for n, m in enumerate(SPLIT_FIELDS) if m // GROUP == i]

        def part_slot(k, n):
            return ((k - 1) * SPLIT + n) % SPLIT_SLOTS

        def split_slot_free(c, k, n):
            same = [s for s in SPLIT_SEQ if part_slot(*s) == part_slot(k, n)]
            before = same.index((k, n)) - 1
            if before < 0:
                if isinstance(c, int) and c == 0:
                    return None
                c = c - 1
            k, n = same[before]
            return group_no(c, group_at(c, k, SPLIT_FIELDS[n] // GROUP)) + 1

        def low_no(c, k, n):
            same = [m for m in range(SPLIT) if LOW_ON_VECTOR[m] == LOW_ON_VECTOR[n]]
            return c * (2 * len(same)) + (k - 1) * len(same) + same.index(n)

        def split_no(c, k, n):
            return c * (2 * SPLIT) + (k - 1) * SPLIT + n

        def low_part(eng, engine, c, k, n, done):
            m = SPLIT_FIELDS[n]
            slot = (NP + group_at(c, k, m // GROUP)) % RING
            eng.wait_ge(hi_ready, split_no(c, k, n) + 1)
            engine.tensor_tensor(out=z_lo[:, part_slot(k, n), :], in0=z[:, slot, m % GROUP, :],
                                 in1=z_hi[:, part_slot(k, n), :].bitcast(f32), op=ALU.subtract).then_inc(done, 1)

        def values_through(c):
            return (c + 1) * 3 + (0 if isinstance(c, int) and c == CHUNKS - 1 else 1)

        def feature_columns(h, n, ks):
            cols = h[:, bass.ds(n * CB + ks[0] * (BATCH - CB), (len(ks) - 1) * (BATCH - CB) + CB)]
            return bass.AP(cols.tensor, cols.offset, [cols.ap[0], [BATCH - CB, len(ks)], [1, CB]])

        def over_bodies(eng, body):
            body(0, True, False)
            with eng.Fori(1, CHUNKS - 1) as c:
                body(c, False, False)
            body(CHUNKS - 1, False, True)

        block = ctx.enter_context(nc.Block())

        @block.gpsimd
        def _(pool):
            nc.gpsimd.memset(ones[:, :], 1.0).then_inc(ones_made, 1)

            def make_rows(c, parity):
                nc.gpsimd.tensor_tensor(out=idx[:, parity, :], in0=ids_sb[:, bass.ds(c * GATHERS, GATHERS)],
                                        in1=base_sb[:, :], op=ALU.add).then_inc(idx_made, 1)

            def start_chunk(c, parity, last=False):
                if not (isinstance(c, int) and c < 1):
                    pool.wait_ge(gather_done, c * (16 * GATHERS))
                if not (isinstance(c, int) and c < 2):
                    pool.wait_ge(scratch_written, (c - 1) * 48)
                pool.wait_ge(idx_made, c + 1)
                if not last:
                    make_rows(c + 1, 1 - parity)

            def gather(parity, j):
                n = 128 if j < GATHERS - 1 else LAST_SLOTS
                nc.gpsimd.indirect_dma_start(
                    out=gathered[0:n, parity, j, :], out_offset=None, in_=table[:, :],
                    in_offset=bass.IndirectOffsetOnAxis(ap=idx[0:n, parity, j:j + 1], axis=0)
                ).then_inc(gather_done, 16)

            def body(c, parity, more=True, last=False):
                if more:
                    start_chunk(c + 2, parity, last)
                lows = [(k, n) for k, n in SPLIT_SEQ if not LOW_ON_VECTOR[n]]
                started = 0
                for at, (k, n) in enumerate(lows):
                    low_part(pool, nc.gpsimd, c, k, n, lo_ready_pool)
                    between = lows[at][0] != lows[at + 1][0] if at + 1 < len(lows) else False
                    count = GATHERS_IN_LAYER0 if between else int(at % GATHER_EVERY == 0)
                    for j in range(started, min(started + count, GATHERS) if more else started):
                        gather(parity, j)
                        started = j + 1
                assert started == (GATHERS if more else 0)

            pool.wait_ge(ids_loaded, 32)
            make_rows(0, 0)
            for c in range(2):
                start_chunk(c, c)
                for j in range(GATHERS):
                    gather(c, j)
            body(0, 0)
            with pool.Fori(1, CHUNKS - 4, 2) as c:
                body(c, 1)
                body(c + 1, 0)
            body(CHUNKS - 3, 1, True, True)
            body(CHUNKS - 2, 0, False)
            body(CHUNKS - 1, 1, False)

        @block.sync
        def _(sp):
            def store_chunk(c, parity):
                g = gathered[:, parity, :, :]
                dst = scratch[bass.ds(c, 1), :, :].rearrange("c n e -> (c n) e")
                full = (GATHERS - 1) * 128
                sp.dma_start(dst[0:full, :].rearrange("(j p) e -> p j e", p=128),
                             g[:, 0:GATHERS - 1, :]).then_inc(scratch_written, 16)
                sp.dma_start(dst[full:full + LAST_SLOTS, :].rearrange("(j p) e -> p j e", p=LAST_SLOTS),
                             g[0:LAST_SLOTS, GATHERS - 1:GATHERS, :]).then_inc(scratch_written, 16)
                sp.dma_start(dst[FIELDS * CB:SCRATCH_FIELDS * CB, :].rearrange("(j p) e -> p j e", p=128),
                             g[:, 0:5, :]).then_inc(scratch_written, 16)

            def chunk_rows(c):
                return scratch[bass.ds(c, 1), :, :].rearrange("c (m b) e -> (c m) (b e)", b=CB)

            def load_pairs(c, p):
                rows = chunk_rows(c)
                tiles = PAIR_GROUPS[p]
                for kk in range(PER_TILE):
                    at = slice(kk * FIELDS, (kk + 1) * FIELDS)
                    if p == 0:
                        sp.dma_start(x_rep[at, :], rows[0:FIELDS, :]).then_inc(pairs_loaded[p], 16)
                    offsets = [PAIR_OFFSETS[PER_TILE * t + kk] for t in tiles if PER_TILE * t + kk < OFFSETS]
                    if offsets:
                        first = rows[offsets[0]:offsets[0] + FIELDS, :]
                        window = bass.AP(first.tensor, first.offset,
                                         [[ROWS, FIELDS], [PER_TILE * ROWS, len(offsets)], [1, ROWS]])
                        sp.dma_start(x_rot[at, tiles[0]:tiles[0] + len(offsets), :],
                                     window).then_inc(pairs_loaded[p], 16)

            def load_fields(c, g):
                rows = chunk_rows(c)[g * GROUP:(g + 1) * GROUP, :].rearrange("m n -> (m n)")
                sp.dma_start(x_all[:, g * GROUP:(g + 1) * GROUP, :].rearrange("p m n -> p (m n)"),
                             rows.partition_broadcast(128)).then_inc(fields_loaded[g], 16)

            sp.dma_start(ids_sb[:, :], idx_in).then_inc(ids_loaded, 16)
            sp.dma_start(base_sb[:, :], base_in).then_inc(ids_loaded, 16)
            sp.wait_ge(gather_done, 16 * GATHERS)
            store_chunk(0, 0)
            sp.wait_ge(scratch_written, 48)
            for p in range(NP):
                load_pairs(0, p)
            for g in range(NG):
                if g == (FIELDS - 2 * STAGE_TILES) // GROUP:
                    sp.wait_ge(w_lo_made, 2)
                load_fields(0, g)
            sp.wait_ge(gather_done, 2 * 16 * GATHERS)
            store_chunk(1, 1)

            def store_features(n, ks):
                sp.wait_ge(h_ready, n + 1)
                sp.dma_start(feature_columns(features, n, ks), ssq[:, ks[0]:ks[-1] + 1, :]).then_inc(h_stored, 16)

            store_features(0, [0])

            def next_chunk(c, more, parity=0):
                sp.wait_ge(z_ready, groups_through(0, c))
                sp.wait_ge(scratch_written, c * 48 + 96)
                for p in range(NP):
                    load_pairs(c + 1, p)
                for g in range(NG):
                    sp.wait_ge(z_ready, group_no(c, group_at(c, 2, g) + 1))
                    load_fields(c + 1, g)
                store_features(c + 1, [0, 1] if isinstance(c, int) and c == 0 else [0, 1, 2])
                if more:
                    sp.wait_ge(gather_done, (c + 3) * (16 * GATHERS))
                    store_chunk(c + 2, parity)

            next_chunk(0, True)
            with sp.Fori(1, CHUNKS - 3, 2) as c:
                next_chunk(c, True, 1)
                next_chunk(c + 1, True, 0)
            next_chunk(CHUNKS - 3, True, 1)
            next_chunk(CHUNKS - 2, False)
            sp.wait_ge(z_ready, groups_through(0, CHUNKS - 1))
            sp.dma_start(top1c_sb, w_top1[3 * 128:3 * 128 + EMB, :]).then_inc(top_loaded, 16)
            sp.dma_start(ctx_sb, ctx_t).then_inc(top_loaded, 16)
            sp.dma_start(top1_sb, w_top1[0:3 * 128, :].rearrange("(k p) n -> p k n", p=128)).then_inc(top_loaded, 16)
            sp.wait_ge(h_stored, CHUNKS * 16)
            for k in range(3):
                cols = slice(k * BATCH, k * BATCH + (CHUNKS - k) * CB)
                sp.dma_start(h0[:, cols], features[:, cols]).then_inc(h_loaded, 16)
            sp.wait_ge(z_ready, group_no(CHUNKS - 1, group_at(CHUNKS - 1, 2, 2) + 1))
            sp.dma_start(top2_sb, w_top2.rearrange("(k p) n -> p k n", p=128)).then_inc(top2_loaded, 16)
            sp.wait_ge(y_done, 1)
            sp.dma_start(out, y_sb[:, :]).then_inc(y_stored, 16)
            sp.wait_ge(y_stored, 16)

        @block.scalar
        def _(act):
            act.dma_start(w0_sb[0:PAIR_ROWS, :, :], w0a).then_inc(w0_loaded, 16)
            act.dma_start(w0b_sb[0:PAIR_ROWS, 0:PAIR_TILES, :], w0b).then_inc(w0_loaded, 16)
            for k, b in enumerate((b0, b1, b2)):
                act.dma_start(bias[:, k:k + 1], b).then_inc(bias_loaded, 16)

            for k, w in ((1, w1), (2, w2)):
                act.dma_start(w_raw[k], w[:, 0:SPLIT, :]).then_inc(w_split_loaded[k], 16)
            act.dma_start(w_sb[1][:, :, :], w1[:, SPLIT:FIELDS, :]).then_inc(w_loaded[1], 16)
            for k in (1, 2):
                act.wait_ge(w_split_loaded[k], 16)
                nc.scalar.activation(w_hi[k][:, :, :], w_raw[k], ACT.Copy).then_inc(w_hi_made, 1)
            act.wait_ge(pairs_loaded[1], PAIR_LOADS[1] * 16)
            act.dma_start(w_sb[2][:, :, :], w2[:, SPLIT:FIELDS, :]).then_inc(w_loaded[2], 16)
            act.dma_start(top3_sb[:, :], w_top3).then_inc(top_bias_loaded, 16)
            act.dma_start(btop1_sb[:, :], b_top1).then_inc(top_bias_loaded, 16)
            act.dma_start(btop2_sb[:, :], b_top2).then_inc(top_bias_loaded, 16)
            act.wait_ge(bias_loaded, 48)

            def layer_sums(k):
                return acc[0][:, :] if k == 0 else u[k][:, :]

            def add_bias(k, c):
                if k == 0:
                    act.wait_ge(z_used, groups_through(0, c))
                else:
                    act.wait_ge(scaled[k], c + 1)
                nc.scalar.activation(t[k], layer_sums(k), ACT.Identity, bias=bias[:, k:k + 1]).then_inc(biased[k], 1)

            def square(k, c):
                if k == 0 and not (isinstance(c, int) and c == 0):
                    act.wait_ge(summed[0], c)
                if k == 2:
                    act.wait_ge(values_summed, values_through(c))
                    nc.scalar.activation(u[2][:, :], t[2], ACT.Square).then_inc(squared[2], 1)
                else:
                    nc.scalar.activation(u[k][:, :], layer_sums(k), ACT.Square,
                                         bias=bias[:, k:k + 1]).then_inc(squared[k], 1)

            def finish(k, c):
                add_bias(k, c)
                square(k, c)

            def roots(n, ks):
                act.wait_ge(norm_done, n + 1)
                if not (isinstance(n, int) and n == 0):
                    act.wait_ge(r_step, n * R_STEPS)
                nc.scalar.activation(root[:, ks[0]:ks[-1] + 1, :],
                                     norm2[:, ks[0] * CB:(ks[-1] + 1) * CB].rearrange("p (k b) -> p k b", b=CB),
                                     ACT.Sqrt).then_inc(root_done, 1)

            def highs(c, k, i):
                for n in splits_of(i):
                    free = split_slot_free(c, k, n)
                    if free is not None:
                        act.wait_ge(z_used, free)
                    act.wait_ge(z_ready, group_no(c, group_at(c, k, i)) + 1)
                    slot = (NP + group_at(c, k, i)) % RING
                    nc.scalar.activation(z_hi[:, part_slot(k, n), :], z[:, slot, SPLIT_FIELDS[n] % GROUP, :],
                                         ACT.Copy).then_inc(hi_ready, 1)

            def body(c, first, last):
                for i in range(NG):
                    highs(c, 1, i)
                    if first and i == 4:
                        roots(0, [0])
                    if i == 3 and not first:
                        add_bias(2, c - 1)
                    if i == 4 and not first:
                        square(2, c - 1)
                finish(1, c)
                for i in range(NG):
                    highs(c, 2, i)
                    if i == 1 and not last:
                        finish(0, c + 1)
                    if i == 8:
                        roots(c + 1, [k for k in range(3) if not (k == 0 and last) and not (k == 2 and first)])

            finish(0, 0)
            over_bodies(act, body)
            finish(2, CHUNKS - 1)
            roots(CHUNKS + 1, [2])

            act.wait_ge(top_bias_loaded, 3 * 16)
            for n in range(TOP1 // 128):
                act.wait_ge(h1_ps, n + 1)
                nc.scalar.activation(h1[:, n, :], top_ps[n][:, :], ACT.Relu,
                                     bias=btop1_sb[:, n:n + 1]).then_inc(h1_done, 1)
            for n in range(TOP2 // 128):
                act.wait_ge(h2_ps, n + 1)
                nc.scalar.activation(h2[:, n, :], acc[n][:, :], ACT.Relu,
                                     bias=btop2_sb[:, n:n + 1]).then_inc(h2_done, 1)
            act.wait_ge(y_ps, 1)
            nc.scalar.copy(y_sb[:, :], acc[2][0:1, :]).then_inc(y_done, 1)

        @block.tensor
        def _(pe):
            def use_group(c, i, k, tiles, chunk):
                g = group_no(c, i)
                slot = (NP + i) % RING
                total = PAIR_TILES if k == 0 else FIELDS
                if tiles[0] == 0 and not (isinstance(chunk, int) and chunk == 0):
                    pe.wait_ge(squared[0] if k == 0 else scaled[k], chunk)
                pe.wait_ge(z_ready, g + 1)
                splits = splits_of(tiles[0] // GROUP) if k else []
                for j, tile in enumerate(tiles[:len(tiles) - len(splits)]):
                    rows = 128 if k else (LAST_PAIR_ROWS if tile == PAIR_TILES - 1 else PAIR_ROWS)
                    w = w_sb[k][:, WHOLE_FIELDS.index(tile), :] if k else w0_sb[0:rows, tile, :]
                    mm = nc.tensor.matmul(acc[k][:, :], w, z[0:rows, slot, j, :],
                                          start=(tile == 0), stop=(tile == total - 1))
                for n in splits:
                    pe.wait_ge(lo_ready_vector if LOW_ON_VECTOR[n] else lo_ready_pool, low_no(c, k, n) + 1)
                    for w, x in ((w_lo, z_hi), (w_hi, z_hi), (w_hi, z_lo)):
                        mm = nc.tensor.matmul(acc[k][:, :], w[k][:, n, :], x[:, part_slot(k, n), :],
                                              start=False, stop=(x is z_lo and SPLIT_FIELDS[n] == FIELDS - 1))
                mm.then_inc(z_used, 1)

            def norms(n, ks, chunks):
                for k, ch in zip(ks, chunks):
                    pe.wait_ge(summed[k], ch + 1)
                if not (isinstance(n, int) and n == 0):
                    pe.wait_ge(r_step, n * R_STEPS)
                nc.tensor.matmul(norm2[:, ks[0] * CB:(ks[-1] + 1) * CB], ones[:, :],
                                 ssq[:, ks[0]:ks[-1] + 1, :].rearrange("p k b -> p (k b)"),
                                 start=True, stop=True).then_inc(norm_done, 1)

            N1, N2 = TOP1 // 128, TOP2 // 128
            feats = [(top1c_sb, ctx_sb)] + \
                    [(top1_sb[:, k, :], h0[:, k * BATCH:(k + 1) * BATCH]) for k in range(3)]

            def top1(n, k):
                w, x = feats[k]
                return nc.tensor.matmul(top_ps[n][:, :], w[:, n * 128:(n + 1) * 128], x, start=(k == 0), stop=(k == 3))

            def top1_early(n):
                for k in range(2):
                    top1(n, k)

            def body(c, first, last):
                if first:
                    pe.wait_ge(w_loaded[1], 16)
                    pe.wait_ge(w_lo_made, 1)
                for at, (k, i) in enumerate(order_of(c)):
                    if first and (k, i) == (2, 0):
                        pe.wait_ge(w_loaded[2], 16)
                        pe.wait_ge(w_lo_made, 2)
                    if last and (k, i) == (2, 0):
                        pe.wait_ge(top_loaded, 3 * 16)
                        pe.wait_ge(h_loaded, 3 * 16)
                        for n in (0, 2):
                            top1_early(n)
                    if first and (k, i) == (1, 3):
                        norms(0, [0], [0])
                    use_group(c, at, k, (CIN_GROUPS if k else PAIR_GROUPS)[i], c if k else c + 1)
                    if (k, i) == (2, 5):
                        ks = [k for k in range(3) if not (k == 0 and last) and not (k == 2 and first)]
                        norms(c + 1, ks, [c + 1 - k for k in ks])

            pe.wait_ge(w0_folded, 2)
            pe.wait_ge(ones_made, 1)
            for i, tiles in enumerate(PAIR_GROUPS):
                use_group(0, i - NP, 0, tiles, 0)
            over_bodies(pe, body)

            for n in (1, 3):
                top1_early(n)
            norms(CHUNKS + 1, [2], [CHUNKS - 1])
            for n in range(N1):
                top1(n, 2)
            pe.wait_ge(h_ready, CHUNKS + 2)
            for n in range(N1):
                top1(n, 3).then_inc(h1_ps, 1)
            pe.wait_ge(top2_loaded, 16)
            pe.wait_ge(top_bias_loaded, 3 * 16)
            for k in range(N1):
                pe.wait_ge(h1_done, k + 1)
                for n in range(N2):
                    mm = nc.tensor.matmul(acc[n][:, :], top2_sb[:, k, n * 128:(n + 1) * 128], h1[:, k, :],
                                          start=(k == 0), stop=(k == N1 - 1))
                    if k == N1 - 1:
                        mm.then_inc(h2_ps, 1)
            for k in range(N2):
                pe.wait_ge(h2_done, k + 1)
                mm = nc.tensor.matmul(acc[2][0:1, :], top3_sb[:, k:k + 1], h2[:, k, :],
                                      start=(k == 0), stop=(k == N2 - 1))
            mm.then_inc(y_ps, 1)

        @block.vector
        def _(dve):
            def make_group(c, i, k, tiles, chunk):
                g = group_no(c, i)
                slot = (NP + i) % RING
                n = len(tiles)
                if not (isinstance(g, int) and g < RING):
                    dve.wait_ge(z_used, g + 1 - RING)
                if k == 0:
                    p = PAIR_GROUPS.index(tiles)
                    dve.wait_ge(pairs_loaded[p], (chunk + 1) * (PAIR_LOADS[p] * 16))
                    rows = LAST_PAIR_ROWS if tiles[-1] == PAIR_TILES - 1 else PAIR_ROWS
                    a = x_rep[0:rows, :]
                    b = x_rot[0:rows, tiles[0]:tiles[0] + n, :]
                else:
                    if k == 1:
                        dve.wait_ge(fields_loaded[tiles[0] // GROUP], (chunk + 1) * 16)
                    if tiles[0] == 0:
                        dve.wait_ge(biased[k - 1], chunk + 1)
                    rows = 128
                    a = t[k - 1]
                    b = x_all[:, tiles[0]:tiles[0] + n, :]
                nc.vector.tensor_tensor(out=z[0:rows, slot, 0:n, :], in0=a.unsqueeze(1).to_broadcast([rows, n, ROWS]),
                                        in1=b, op=ALU.mult).then_inc(z_ready, 1)

            def weights_low(k):
                dve.wait_ge(w_hi_made, k)
                nc.vector.tensor_tensor(out=w_lo[k][:, :, :], in0=w_raw[k], in1=w_hi[k][:, :, :].bitcast(f32),
                                        op=ALU.subtract).then_inc(w_lo_made, 1)

            def lows(c, k, i):
                for n in splits_of(i):
                    if LOW_ON_VECTOR[n]:
                        low_part(dve, nc.vector, c, k, n, lo_ready_vector)

            def scale(k, c, n):
                dve.wait_ge(z_used, groups_through(k, c))
                dve.wait_ge(r_step, n * R_STEPS)
                nc.vector.tensor_tensor(
                    out=u[k][:, :].rearrange("p (b e) -> p b e", e=EMB),
                    in0=acc[k][:, :].rearrange("p (b e) -> p b e", e=EMB),
                    in1=r[:, k - 1, :].unsqueeze(2).to_broadcast([128, CB, EMB]), op=ALU.mult).then_inc(scaled[k], 1)

            def sum_values(k, c):
                dve.wait_ge(biased[k], c + 1)
                nc.vector.tensor_reduce(dsum[:, k, :], t[k].rearrange("p (b e) -> p b e", e=EMB),
                                        AX.X, ALU.add).then_inc(values_summed, 1)

            def sum_squares(k, c):
                dve.wait_ge(squared[k], c + 1)
                nc.vector.tensor_reduce(ssq[:, k, :], u[k][:, :].rearrange("p (b e) -> p b e", e=EMB),
                                        AX.X, ALU.add).then_inc(summed[k], 1)

            def reciprocals(n, ks):
                s = slice(ks[0], ks[-1] + 1)
                sq = norm2[:, ks[0] * CB:(ks[-1] + 1) * CB].rearrange("p (k b) -> p k b", b=CB)
                dve.wait_ge(root_done, n + 1)
                nc.vector.reciprocal(r[:, s, :], root[:, s, :]).then_inc(r_step, 1)
                dve.wait_ge(r_step, n * R_STEPS + 1)
                nc.vector.scalar_tensor_tensor(out=root[:, s, :], in0=sq, scalar=F32_MAX, in1=r[:, s, :],
                                               op0=ALU.min, op1=ALU.mult).then_inc(r_step, 1)
                dve.wait_ge(r_step, n * R_STEPS + 2)
                nc.vector.scalar_tensor_tensor(out=root[:, s, :], in0=root[:, s, :], scalar=-0.5, in1=r[:, s, :],
                                               op0=ALU.mult, op1=ALU.mult).then_inc(r_step, 1)
                dve.wait_ge(r_step, n * R_STEPS + 3)
                nc.vector.scalar_tensor_tensor(out=r[:, s, :], in0=root[:, s, :], scalar=1.5, in1=r[:, s, :],
                                               op0=ALU.add, op1=ALU.mult).then_inc(r_step, 1)
                dve.wait_ge(r_step, n * R_STEPS + 4)
                if isinstance(n, int) and n >= CHUNKS:
                    feats = feature_columns(h0, n, ks)
                else:
                    feats = ssq[:, s, :]
                nc.vector.tensor_tensor(out=feats, in0=r[:, s, :], in1=dsum[:, s, :], op=ALU.mult).then_inc(h_ready, 1)

            def body(c, first, last):
                ks = [k for k in range(3) if not (k == 0 and last) and not (k == 2 and first)]
                for at, (k, i) in enumerate(order_of(c)):
                    if (k, i) == (2, 0):
                        scale(1, c, c + 1)
                    make_group(c, at, k, (CIN_GROUPS if k else PAIR_GROUPS)[i], c if k else c + 1)
                    if k:
                        lows(c, k, i - 1)
                        if i == NG - 1:
                            lows(c, k, i)
                    if first and (k, i) == (1, 0):
                        sum_values(0, 0)
                        sum_squares(0, 0)
                    if first and (k, i) == (1, 7):
                        reciprocals(0, [0])
                    if (k, i) == (1, 3) and not first:
                        scale(2, c - 1, c + 1)
                    if (k, i) == (1, 4) and not first:
                        sum_values(2, c - 1)
                    if (k, i) == (1, 6) and not first:
                        dve.wait_ge(h_stored, (c + 1) * 16)
                        sum_squares(2, c - 1)
                    if (k, i) == (2, 1):
                        if first:
                            dve.wait_ge(h_stored, 16)
                        sum_values(1, c)
                        sum_squares(1, c)
                    if (k, i) == (2, 3) and not last:
                        sum_values(0, c + 1)
                        sum_squares(0, c + 1)
                    if (k, i) == (2, 10):
                        reciprocals(c + 1, ks)

            dve.wait_ge(w0_loaded, 32)
            full = slice(0, PAIR_TILES - 1)
            nc.vector.tensor_tensor(out=w0_sb[0:PAIR_ROWS, full, :], in0=w0_sb[0:PAIR_ROWS, full, :],
                                    in1=w0b_sb[0:PAIR_ROWS, full, :], op=ALU.add).then_inc(w0_folded, 1)
            nc.vector.tensor_tensor(out=w0_sb[0:FIELDS, PAIR_TILES - 1, :], in0=w0_sb[0:FIELDS, PAIR_TILES - 1, :],
                                    in1=w0b_sb[0:FIELDS, PAIR_TILES - 1, :], op=ALU.add).then_inc(w0_folded, 1)
            dve.wait_ge(w0_folded, 2)
            weights_low(1)
            weights_low(2)
            for i, tiles in enumerate(PAIR_GROUPS):
                make_group(0, i - NP, 0, tiles, 0)
            over_bodies(dve, body)
            scale(2, CHUNKS - 1, CHUNKS + 1)
            sum_values(2, CHUNKS - 1)
            sum_squares(2, CHUNKS - 1)
            reciprocals(CHUNKS + 1, [2])


def kernel(**inputs):
    import concourse.bacc as bacc
    from concourse.bass_utils import run_bass_kernel_spmd

    def lay(a):
        return np.ascontiguousarray(a)

    tables = [np.asarray(inputs[f"tbl_{f}"]) for f in range(FIELDS)]
    starts = np.concatenate([[0], np.cumsum([a.shape[0] for a in tables])])[:FIELDS].astype(np.int32)
    slot_fields = GATHERS * SLOT_FIELDS

    def slots(a):
        a = a.reshape(CHUNKS, CB, FIELDS).transpose(0, 2, 1)
        a = np.concatenate([a, np.zeros((CHUNKS, slot_fields - FIELDS, CB), a.dtype)], axis=1)
        a = a.reshape(CHUNKS, GATHERS, SLOT_FIELDS * CB)
        return lay(a.transpose(2, 0, 1).reshape(128, CHUNKS * GATHERS))

    order_a = np.zeros((PAIR_ROWS, PAIR_TILES), np.int64)
    order_b = np.zeros((PAIR_ROWS, PAIR_TILES), np.int64)
    for n, k in enumerate(PAIR_OFFSETS):
        for i in range(FIELDS):
            j = (i + k) % FIELDS
            at = (n % PER_TILE * FIELDS + i, n // PER_TILE)
            order_a[at], order_b[at] = i * FIELDS + j, j * FIELDS + i
    w0 = np.asarray(inputs["L0_rec_w0"])

    def fields_first(w):
        return lay(w.reshape(FIELDS, UNITS, UNITS).transpose(1, 0, 2)[:, WEIGHT_ORDER, :])

    arrays = {
        "ids": slots(np.asarray(inputs["ids"])),
        "bases": lay(slots(np.broadcast_to(starts, (BATCH, FIELDS)))[:, 0:GATHERS]),
        "table": lay(np.concatenate(tables, axis=0)),
        "ctx_t": lay(np.asarray(inputs["dense_ctx"]).T),
        "w0a": lay(w0[order_a]),
        "w0b": lay(w0[order_b]),
        "w1": fields_first(np.asarray(inputs["L0_rec_w1"])),
        "w2": fields_first(np.asarray(inputs["L0_rec_w2"])),
        "b0": lay(np.asarray(inputs["L0_rec_b0"]).reshape(UNITS, 1)),
        "b1": lay(np.asarray(inputs["L0_rec_b1"]).reshape(UNITS, 1)),
        "b2": lay(np.asarray(inputs["L0_rec_b2"]).reshape(UNITS, 1)),
        "w_top1": lay(inputs["W_top1"]),
        "b_top1": lay(np.asarray(inputs["b_top1"]).reshape(TOP1 // 128, 128).T),
        "w_top2": lay(inputs["W_top2"]),
        "b_top2": lay(np.asarray(inputs["b_top2"]).reshape(TOP2 // 128, 128).T),
        "w_top3": lay(np.asarray(inputs["W_top3"]).reshape(TOP2 // 128, 128).T),
    }
    nc = bacc.Bacc("TRN2", target_bir_lowering=False, num_devices=1, dynamic_dma_scratch_size=DMA_SCRATCH)
    args = [nc.dram_tensor(f"in_{name}", a.shape, mybir.dt.from_np(a.dtype), kind="ExternalInput").ap()
            for name, a in arrays.items()]
    args.append(nc.dram_tensor("scores", (1, BATCH), mybir.dt.float32, kind="ExternalOutput").ap())
    cin_kernel(nc, *args)
    got = run_bass_kernel_spmd(nc, [{f"in_{name}": a for name, a in arrays.items()}], core_ids=[0])
    return got.results[0]["scores"].reshape(BATCH, 1)
```
